# Optimizing a Trainium2 kernel written in Bass

```python
import numpy as np
import jax
import jax.numpy as jnp

def _softmax(x, axis=-1):
    return jax.nn.softmax(x, axis=axis)

def _gelu(x):
    return jax.nn.gelu(x, approximate=True)

def _silu(x):
    return jax.nn.silu(x)

def _sigmoid(x):
    return jax.nn.sigmoid(x)

def _layernorm(x, axis=-1, eps=1e-05):
    m = jnp.mean(x, axis=axis, keepdims=True)
    v = jnp.var(x, axis=axis, keepdims=True)
    return (x - m) / jnp.sqrt(v + eps)

def _scatter_add(tgt, idx, src, axis=0):
    return tgt.at[idx].add(src)

def _segment_sum(src, seg, n):
    return jax.ops.segment_sum(src, seg, n)
kernel_name = 'mk_prb_d2_jaxref_r8_f3952d'

def setup_inputs(seed: int=0):
    np.random.seed(seed)
    _w = jnp.asarray

    def _L0_attn_setup():
        import jax, jax.numpy as jnp
        import numpy as np
        import math
        DIM = 128
        NUM_HEADS = 16
        HEAD_DIM = DIM // NUM_HEADS
        BATCH = 4
        SEQ = 512

        def _feature_map(x, R):
            x = x / math.sqrt(HEAD_DIM)
            proj = jnp.einsum('bhnd,dm->bhnm', x, R)
            sq_norm = jnp.sum(x * x, axis=-1, keepdims=True)
            return jnp.exp(proj - 0.5 * sq_norm)
        key = jax.random.key(seed)
        ks = jax.random.split(key, 10)
        s = 1.0 / math.sqrt(DIM)
        return {'x': jax.random.normal(ks[0], (BATCH, SEQ, DIM), dtype=jnp.float32), 'Wq': jax.random.normal(ks[1], (DIM, DIM), dtype=jnp.float32) * s, 'bq': jax.random.normal(ks[2], (DIM,), dtype=jnp.float32) * 0.01, 'Wk': jax.random.normal(ks[3], (DIM, DIM), dtype=jnp.float32) * s, 'bk': jax.random.normal(ks[4], (DIM,), dtype=jnp.float32) * 0.01, 'Wv': jax.random.normal(ks[5], (DIM, DIM), dtype=jnp.float32) * s, 'bv': jax.random.normal(ks[6], (DIM,), dtype=jnp.float32) * 0.01, 'Wo': jax.random.normal(ks[7], (DIM, DIM), dtype=jnp.float32) * s, 'bo': jax.random.normal(ks[8], (DIM,), dtype=jnp.float32) * 0.01, 'R': jax.random.normal(ks[9], (HEAD_DIM, HEAD_DIM), dtype=jnp.float32) * 0.4}
    _L0_attn_in = _L0_attn_setup()

    def _L0_ffn_setup():
        import jax, jax.numpy as jnp
        import numpy as np
        B, T, D, F, E = (2, 128, 128, 512, 8)
        EPS = 1e-06
        key = jax.random.key(seed)
        k = jax.random.split(key, 5)
        scale = 0.02
        return {'x': jax.random.normal(k[0], (B, T, D), dtype=jnp.float32), 'rms_w': jnp.ones((D,), dtype=jnp.float32), 'gate_w': jax.random.normal(k[1], (E, D), dtype=jnp.float32) * scale, 'W1': jax.random.normal(k[2], (E, D, F), dtype=jnp.float32) * scale, 'b1': jnp.zeros((E, F), dtype=jnp.float32), 'W2': jax.random.normal(k[3], (E, F, D), dtype=jnp.float32) * scale, 'b2': jnp.zeros((E, D), dtype=jnp.float32)}
    _L0_ffn_in = _L0_ffn_setup()

    def _L1_attn_setup():
        import jax, jax.numpy as jnp
        import numpy as np
        B, T, D = (2, 256, 128)
        H = 16
        HD = D // H
        DL = 64
        NR = 64
        EPS = 1.1920929e-07

        def _rms_norm(x, w):
            ms = jnp.mean(jnp.square(x), axis=-1, keepdims=True)
            return x * jax.lax.rsqrt(ms + EPS) * w
        key = jax.random.key(seed)
        ks = jax.random.split(key, 10)
        s = 0.02
        return {'x': jax.random.normal(ks[0], (B, T, D), dtype=jnp.float32), 'W_DQ': jax.random.normal(ks[1], (DL, HD), dtype=jnp.float32) * s, 'W_UQ': jax.random.normal(ks[2], (HD, DL), dtype=jnp.float32) * s, 'W_DKV': jax.random.normal(ks[3], (2 * DL, HD), dtype=jnp.float32) * s, 'W_UKV': jax.random.normal(ks[4], (2 * HD, 2 * DL), dtype=jnp.float32) * s, 'W_QR': jax.random.normal(ks[5], (NR, HD), dtype=jnp.float32) * s, 'W_KR': jax.random.normal(ks[6], (NR, HD), dtype=jnp.float32) * s, 'W_O': jax.random.normal(ks[7], (HD, HD), dtype=jnp.float32) * s, 'q_norm_w': jnp.ones((HD,), dtype=jnp.float32), 'k_norm_w': jnp.ones((HD,), dtype=jnp.float32)}
    _L1_attn_in = _L1_attn_setup()

    def _L1_ffn_setup():
        import jax, jax.numpy as jnp
        import numpy as np
        E = 8
        EPS = 1e-05
        key = jax.random.key(seed)
        ks = jax.random.split(key, 6)
        d, f = (128, 512)
        B, S = (2, 128)
        x = jax.random.normal(ks[0], (B, S, d), dtype=jnp.float32)
        c = jax.random.normal(ks[1], (d, E), dtype=jnp.float32)
        q, _ = jnp.linalg.qr(c)
        centroids = (0.1 * q.T).astype(jnp.float32)
        w1 = jax.random.normal(ks[2], (E, d, f), dtype=jnp.float32) / np.sqrt(d).astype(np.float32)
        b1 = jnp.zeros((E, f), dtype=jnp.float32)
        w2 = jax.random.normal(ks[3], (E, f, d), dtype=jnp.float32) * 0.02
        b2 = jnp.zeros((E, d), dtype=jnp.float32)
        gamma = jnp.ones((E, d), dtype=jnp.float32)
        beta = jnp.zeros((E, d), dtype=jnp.float32)
        return dict(x=x, centroids=centroids, w1=w1, b1=b1, w2=w2, b2=b2, gamma=gamma, beta=beta)
    _L1_ffn_in = _L1_ffn_setup()
    _d = {'L0_attn_x': _L0_attn_in['x'], 'L0_attn_Wq': _L0_attn_in['Wq'], 'L0_attn_bq': _L0_attn_in['bq'], 'L0_attn_Wk': _L0_attn_in['Wk'], 'L0_attn_bk': _L0_attn_in['bk'], 'L0_attn_Wv': _L0_attn_in['Wv'], 'L0_attn_bv': _L0_attn_in['bv'], 'L0_attn_Wo': _L0_attn_in['Wo'], 'L0_attn_bo': _L0_attn_in['bo'], 'L0_attn_R': _L0_attn_in['R'], 'L0_ffn_rms_w': _L0_ffn_in['rms_w'], 'L0_ffn_gate_w': _L0_ffn_in['gate_w'], 'L0_ffn_W1': _L0_ffn_in['W1'], 'L0_ffn_b1': _L0_ffn_in['b1'], 'L0_ffn_W2': _L0_ffn_in['W2'], 'L0_ffn_b2': _L0_ffn_in['b2'], 'L1_attn_W_DQ': _L1_attn_in['W_DQ'], 'L1_attn_W_UQ': _L1_attn_in['W_UQ'], 'L1_attn_W_DKV': _L1_attn_in['W_DKV'], 'L1_attn_W_UKV': _L1_attn_in['W_UKV'], 'L1_attn_W_QR': _L1_attn_in['W_QR'], 'L1_attn_W_KR': _L1_attn_in['W_KR'], 'L1_attn_W_O': _L1_attn_in['W_O'], 'L1_attn_q_norm_w': _L1_attn_in['q_norm_w'], 'L1_attn_k_norm_w': _L1_attn_in['k_norm_w'], 'L1_ffn_centroids': _L1_ffn_in['centroids'], 'L1_ffn_w1': _L1_ffn_in['w1'], 'L1_ffn_b1': _L1_ffn_in['b1'], 'L1_ffn_w2': _L1_ffn_in['w2'], 'L1_ffn_b2': _L1_ffn_in['b2'], 'L1_ffn_gamma': _L1_ffn_in['gamma'], 'L1_ffn_beta': _L1_ffn_in['beta']}
    _x0 = _d['L0_attn_x']
    _d['L0_attn_x'] = jax.random.normal(jax.random.fold_in(jax.random.key(seed), 1), (16, 512, 128), dtype=_x0.dtype)
    del _x0
    return _d

def reference(L0_attn_x, L0_attn_Wq, L0_attn_bq, L0_attn_Wk, L0_attn_bk, L0_attn_Wv, L0_attn_bv, L0_attn_Wo, L0_attn_bo, L0_attn_R, L0_ffn_rms_w, L0_ffn_gate_w, L0_ffn_W1, L0_ffn_b1, L0_ffn_W2, L0_ffn_b2, L1_attn_W_DQ, L1_attn_W_UQ, L1_attn_W_DKV, L1_attn_W_UKV, L1_attn_W_QR, L1_attn_W_KR, L1_attn_W_O, L1_attn_q_norm_w, L1_attn_k_norm_w, L1_ffn_centroids, L1_ffn_w1, L1_ffn_b1, L1_ffn_w2, L1_ffn_b2, L1_ffn_gamma, L1_ffn_beta):

    def _L0_attn_ref(x, Wq, bq, Wk, bk, Wv, bv, Wo, bo, R):
        import jax, jax.numpy as jnp
        import numpy as np
        import math
        DIM = 128
        NUM_HEADS = 16
        HEAD_DIM = DIM // NUM_HEADS
        BATCH = 4
        SEQ = 512

        def _feature_map(x, R):
            x = x / math.sqrt(HEAD_DIM)
            proj = jnp.einsum('bhnd,dm->bhnm', x, R)
            sq_norm = jnp.sum(x * x, axis=-1, keepdims=True)
            return jnp.exp(proj - 0.5 * sq_norm)
        b, n, _ = x.shape
        h, d = (NUM_HEADS, HEAD_DIM)

        def split_heads(t):
            return t.reshape(b, n, h, d).transpose(0, 2, 1, 3)
        q = split_heads(x @ Wq.T + bq)
        k = split_heads(x @ Wk.T + bk)
        v = split_heads(x @ Wv.T + bv)
        q_prime = _feature_map(q, R)
        k_prime = _feature_map(k, R)
        kv = jnp.einsum('bhnd,bhne->bhde', k_prime, v)
        z = 1.0 / (jnp.sum(q_prime, axis=-1) + 1e-08)
        out = jnp.einsum('bhnd,bhde,bhn->bhne', q_prime, kv, z)
        out = out.transpose(0, 2, 1, 3).reshape(b, n, DIM)
        return out @ Wo.T + bo

    def _L0_ffn_ref(x, rms_w, gate_w, W1, b1, W2, b2):
        import jax, jax.numpy as jnp
        import numpy as np
        B, T, D, F, E = (2, 128, 128, 512, 8)
        EPS = 1e-06
        ms = jnp.mean(x * x, axis=-1, keepdims=True)
        xn = x * jax.lax.rsqrt(ms + EPS) * rms_w
        logits = jnp.einsum('btd,ed->bte', xn, gate_w)
        scores = jax.nn.softmax(logits, axis=-1)
        top1_idx = jnp.argmax(scores, axis=-1)
        top1_score = jnp.max(scores, axis=-1)
        out = jnp.zeros_like(xn)
        for e in range(E):
            h = jax.nn.silu(jnp.einsum('btd,df->btf', xn, W1[e]) + b1[e])
            ye = jnp.einsum('btf,fd->btd', h, W2[e]) + b2[e]
            out = jnp.where((top1_idx == e)[..., None], ye, out)
        return out * top1_score[..., None]

    def _L1_attn_ref(x, W_DQ, W_UQ, W_DKV, W_UKV, W_QR, W_KR, W_O, q_norm_w, k_norm_w):
        import jax, jax.numpy as jnp
        import numpy as np
        B, T, D = (2, 256, 128)
        H = 16
        HD = D // H
        DL = 64
        NR = 64
        EPS = 1.1920929e-07

        def _rms_norm(x, w):
            ms = jnp.mean(jnp.square(x), axis=-1, keepdims=True)
            return x * jax.lax.rsqrt(ms + EPS) * w
        b, t, d = x.shape
        scale = HD ** (-0.5)
        xh = x.reshape(b, t, H, HD).transpose(0, 2, 1, 3)
        c_q = jnp.einsum('bhtd,ld->bhtl', xh, W_DQ)
        q_c = jnp.einsum('bhtl,dl->bhtd', c_q, W_UQ)
        q_c_norm = _rms_norm(q_c, q_norm_w)
        q_r = jnp.einsum('bhtd,rd->bhtr', q_c_norm, W_QR)
        q = jnp.concatenate([q_c_norm, q_r], axis=-1)
        c_kv = jnp.einsum('bhtd,ld->bhtl', xh, W_DKV)
        kv = jnp.einsum('bhtl,dl->bhtd', c_kv, W_UKV)
        k_c, v_c = (kv[..., :HD], kv[..., HD:])
        k_c_norm = _rms_norm(k_c, k_norm_w)
        k_r = jnp.einsum('bhtd,rd->bhtr', xh, W_KR)
        k = jnp.concatenate([k_c_norm, k_r], axis=-1)
        scores = jnp.einsum('bhqd,bhkd->bhqk', q, k) * scale
        causal = jnp.triu(jnp.full((t, t), -jnp.inf, dtype=scores.dtype), k=1)
        attn = jax.nn.softmax(scores + causal, axis=-1)
        ctx = jnp.einsum('bhqk,bhkd->bhqd', attn, v_c)
        out = jnp.einsum('bhtd,od->bhto', ctx, W_O)
        return out.transpose(0, 2, 1, 3).reshape(b, t, d)

    def _L1_ffn_ref(x, centroids, w1, b1, w2, b2, gamma, beta):
        import jax, jax.numpy as jnp
        import numpy as np
        E = 8
        EPS = 1e-05
        B, S, d = x.shape
        feats = x.reshape(-1, d)
        aff = feats @ centroids.T
        eid = jnp.argmax(aff, axis=1)
        mu = jnp.mean(feats, axis=-1, keepdims=True)
        var = jnp.var(feats, axis=-1, keepdims=True)
        xhat = (feats - mu) * jax.lax.rsqrt(var + EPS)
        out = jnp.zeros_like(feats)
        for e in range(E):
            mask = (eid == e).astype(feats.dtype)[:, None]
            h = xhat * gamma[e] + beta[e]
            y = feats + jax.nn.relu(h @ w1[e] + b1[e]) @ w2[e] + b2[e]
            alpha = jax.nn.sigmoid(feats @ centroids[e])[:, None]
            out = out + mask * (alpha * y + (1.0 - alpha) * feats)
        return out.reshape(B, S, d)
    x = L0_attn_x
    xn = _layernorm(x, axis=-1)
    x = x + _L0_attn_ref(xn, L0_attn_Wq, L0_attn_bq, L0_attn_Wk, L0_attn_bk, L0_attn_Wv, L0_attn_bv, L0_attn_Wo, L0_attn_bo, L0_attn_R) + _L0_ffn_ref(xn, L0_ffn_rms_w, L0_ffn_gate_w, L0_ffn_W1, L0_ffn_b1, L0_ffn_W2, L0_ffn_b2)
    xn = _layernorm(x, axis=-1)
    x = x + _L1_attn_ref(xn, L1_attn_W_DQ, L1_attn_W_UQ, L1_attn_W_DKV, L1_attn_W_UKV, L1_attn_W_QR, L1_attn_W_KR, L1_attn_W_O, L1_attn_q_norm_w, L1_attn_k_norm_w) + _L1_ffn_ref(xn, L1_ffn_centroids, L1_ffn_w1, L1_ffn_b1, L1_ffn_w2, L1_ffn_b2, L1_ffn_gamma, L1_ffn_beta)
    return x

_drawn_inputs = setup_inputs


def setup_inputs(seed=0):
    import zlib

    import numpy as np

    out = dict(_drawn_inputs(seed))
    spreads = {'L0_ffn_rms_w': (1.0, 0.6),
     'L0_ffn_b1': (0.0, 0.8),
     'L0_ffn_b2': (0.0, 0.8),
     'L1_attn_q_norm_w': (1.0, 0.6),
     'L1_attn_k_norm_w': (1.0, 0.6),
     'L1_ffn_b1': (0.0, 0.8),
     'L1_ffn_b2': (0.0, 2.0),
     'L1_ffn_gamma': (1.0, 0.6),
     'L1_ffn_beta': (0.0, 0.8)}
    factors = {'L0_attn_bq': 8.0,
     'L0_attn_bk': 8.0,
     'L0_attn_bo': 8.0,
     'L0_ffn_gate_w': 8.0,
     'L0_ffn_W1': 8.0,
     'L0_ffn_W2': 8.0,
     'L1_attn_W_DQ': 64.0,
     'L1_attn_W_UQ': 64.0,
     'L1_attn_W_DKV': 35.573,
     'L1_attn_W_UKV': 32.6,
     'L1_attn_W_QR': 64.0,
     'L1_attn_W_KR': 64.0,
     'L1_attn_W_O': 25.803,
     'L1_ffn_centroids': 5.3,
     'L1_ffn_w1': 6.678,
     'L1_ffn_w2': 5.446}
    for name, (base, spread) in spreads.items():
        noise = np.random.default_rng([zlib.crc32(name.encode()), seed]).standard_normal(out[name].shape)
        drawn = base * np.exp(spread * noise) if base else spread * noise
        out[name] = jnp.asarray(drawn.astype(out[name].dtype))
    for name, factor in factors.items():
        out[name] = (out[name] * factor).astype(out[name].dtype)
    return out
```

```python
from contextlib import ExitStack

import numpy as np

import concourse.bass as bass
from concourse import mybir

F32 = mybir.dt.float32
BF16 = mybir.dt.bfloat16
I32 = mybir.dt.int32
ALU = mybir.AluOpType
ACT = mybir.ActivationFunctionType
AX_X = mybir.AxisListType.X

P = 128
D = 128
SEQ = 512
BATCHES = 16
TPB = SEQ // P
TILES = BATCHES * TPB
HEADS = 16
HD = D // HEADS
PAIRS = HEADS // 2
QUADS = HEADS // 4
E = 8
F = 512
FC = F // P
SLOT_TILES = TILES + E
HEAD = 2
X_LOADS = 4
LOW = -1e30
PARTS = [(0, 0), (1, 0), (2, 0), (0, 1), (1, 1), (0, 2)]
K_STACK = len(PARTS) * HD
K_FULL = K_STACK + 3
ARENA = 17200
LN_EPS = 1e-5
RMS_EPS0 = 1e-6
RMS_EPS1 = 1.1920929e-07
FFN_EPS1 = 1e-5


def expert_of(eng, reg, table, tile):
    eng.reg_load(reg, table[0:1, bass.ds(tile, 1)])
    return eng.snap(reg, min_val=0, max_val=E - 1)


class Count:

    def __init__(self, handle, per, head=HEAD):
        self.handle, self.per, self.head = handle, per, head

    def at(self, k, c):
        return k * self.per + (self.per * self.head + c)

    def start(self, eng):
        eng.sem_inc(self.handle, self.per * self.head)


def steps(eng, items, depth, body, peel=0):
    begin = max(depth + depth % 2, peel)
    turns = (items - begin) // 2
    flags = lambda t: [0 <= t - s < items for s in range(depth + 1)]
    for t in range(begin):
        body(t, t % 2, t // 2, flags(t))
    if turns == 1:
        for u in range(2):
            body(begin + u, u, begin // 2, flags(begin + u))
    elif turns > 1:
        with eng.Fori(0, turns) as turn:
            for u in range(2):
                body(turn * 2 + (begin + u), u, turn + begin // 2, [True] * (depth + 1))
    for t in range(begin + 2 * turns, items + depth):
        body(t, t % 2, t // 2, flags(t))


def build(nc, x, Wq, bq, Wk, bk, Wv, bv, Wo, bo, R, rms_w, gate_w, W1, b1, W2, b2,
          W_DQ, W_UQ, W_DKV, W_UKV, W_QR, W_KR, W_O, q_norm_w, k_norm_w,
          centroids, w1, fb1, w2, fb2, gamma, beta, out):
    ctx = ExitStack()
    with ctx:
        def sb(name, shape, dt=F32):
            return ctx.enter_context(nc.sbuf_tensor(name, shape, dt))

        def sem(name):
            return ctx.enter_context(nc.semaphore(name))

        def count(name, per=1, head=HEAD):
            return Count(sem(name), per, head)

        bank = [ctx.enter_context(nc.psum_tensor(f"bank{i}", [P, 512], F32)) for i in range(8)]

        sorted_x = nc.dram_tensor("sorted_x", (SLOT_TILES * P, D), F32, kind="Internal").ap()
        sorted_y = nc.dram_tensor("sorted_y", (SLOT_TILES * P, D), F32, kind="Internal").ap()
        parts_d = [nc.dram_tensor(f"parts_d{u}", (P, 6, SEQ), BF16, kind="Internal").ap() for u in range(2)]
        mrow_d = [nc.dram_tensor(f"mrow_d{h}", (24, SEQ), BF16, kind="Internal").ap() for h in range(2)]

        X = sb("X", [P, TILES, D])
        W1s = sb("W1s", [P, E * F])
        W2s = sb("W2s", [P, E * FC * D])
        b1T = sb("b1T", [P, E * FC])
        b1L = [sb(f"b1L{l}", [E * FC, P]) for l in range(2)]
        b2bc = sb("b2bc", [P, E * D])
        ident = sb("ident", [P, P])
        identb = sb("identb", [P, P], BF16)
        tri = sb("tri", [P, P], BF16)
        onesb = sb("onesb", [P, P], BF16)
        blk = sb("blk", [P, P])
        sqblk = sb("sqblk", [P, P])
        maskT = sb("maskT", [P, P], BF16)
        maskS = sb("maskS", [P, SEQ])
        ones512 = sb("ones512", [P, 512])
        zeros512 = sb("zeros512", [P, 512])
        iotaE = sb("iotaE", [P, E])
        iotaJ = sb("iotaJ", [P, SLOT_TILES])
        wn = sb("wn", [P, 4, P])
        wT = sb("wT", [P, 4, P])
        vecs = sb("vecs", [P, 8])
        bvo = sb("bvo", [P, 2, D])
        Rn = sb("Rn", [HD, HD])
        Rblk = sb("Rblk", [P, P])
        gln = sb("gln", [E, 2, D])
        glT = sb("glT", [P, 2, E])
        gb = sb("gb", [2 * E, D])
        gbT = sb("gbT", [P, 2 * E])
        Pb = sb("Pb", [P, 4, SEQ])
        setup_space = Pb[:, :, :].rearrange("p a n -> p (a n)")
        wsm = setup_space[:, 0:6 * P].rearrange("p (a n) -> p a n", n=P)
        wrep = setup_space[:, 6 * P:14 * P].rearrange("p (a n) -> p a n", n=P)
        PROJ = sb("PROJ", [P, 4 * P])
        nrm8 = sb("nrm8", [HD, 2])
        kwbc = sb("kwbc", [P, HD])
        MV = sb("MV", [P, TILES, 2])
        RS = sb("RS", [P, TILES])
        R2 = sb("R2", [P, TILES])
        tmp64 = sb("tmp64", [P, 4, TILES])
        LG = sb("LG", [P, TILES, E])
        ohE = sb("ohE", [P, E, TILES], BF16)
        rt = sb("rt", [P, 3, E * TILES])
        rs8 = sb("rs8", [P, 8, E])
        rs8i = sb("rs8i", [P, E], I32)
        rj = sb("rj", [P, SLOT_TILES, E])
        rjs = sb("rjs", [P, SLOT_TILES])
        EID = sb("EID", [P, SLOT_TILES], I32)
        POS = sb("POS", [P, TILES], I32)
        SC = sb("SC", [P, TILES])
        xs = sb("xs", [P, 2, TPB * D])
        xr = sb("xr", [P, 2, TPB * D])
        idx = sb("idx", [P, 2, TPB], I32)
        xT = sb("xT", [P, 2, SEQ])
        st6 = sb("st6", [P, TPB, 6])
        mv4 = sb("mv4", [P, TPB, 2])
        yg = xr
        arena = sb("arena", [P, ARENA])
        at_ = [0]

        def carve(n, dt=F32):
            a = at_[0]
            at_[0] += n
            assert at_[0] <= ARENA, at_[0]
            v = arena[:, a:a + n]
            return v if dt == F32 else v.bitcast(dt)

        qT = carve(SEQ); kT = carve(SEQ); qsq = carve(SEQ); ksq = carve(SEQ)
        v_s = [carve(SEQ) for _ in range(2)]
        qp = carve(SEQ); kp = carve(SEQ)
        qz = carve(SEQ); qzT = carve(SEQ)
        qs = carve(TPB * HEADS); qr = carve(TPB * HEADS)
        kvm = carve(P); kvo = carve(P); ot = carve(SEQ)
        at_[0] = 0
        xin = [carve(P) for _ in range(2)]
        xinT = [carve(P) for _ in range(2)]
        hs = [carve(F) for _ in range(2)]
        hb = [carve(F) for _ in range(2)]
        ha = [carve(F) for _ in range(2)]
        ys = [carve(D) for _ in range(2)]
        at_[0] = 0
        raw = carve(TPB * 384).rearrange("p (t c) -> p t c", t=TPB)
        vst = carve(TPB * D).rearrange("p (t c) -> p t c", t=TPB)
        sq = carve(TPB * 256)
        ms = carve(P); rq = carve(P); rt1 = carve(P); rln = carve(P)
        qn = carve(SEQ); kn = carve(SEQ)
        r1 = carve(2 * SEQ).rearrange("p (a n) -> p a n", a=2)
        parts = carve(6 * SEQ // 2, BF16).rearrange("p (a n) -> p a n", a=6)
        qst = [carve(PAIRS * SEQ // 2, BF16).rearrange("p (a n) -> p a n", a=PAIRS) for _ in range(2)]
        kst = [carve(PAIRS * SEQ // 2, BF16).rearrange("p (a n) -> p a n", a=PAIRS) for _ in range(2)]
        mrowT = [carve(SEQ // 2, BF16) for _ in range(2)]
        MX = carve(HEADS * TPB)
        mr = carve(3 * 32)
        att = carve(SEQ)
        OTs = carve(SEQ)
        rden = carve(HEADS)
        mparts = carve(2 * 3 * 8 * TPB // 2, BF16)
        vaug = sb("vaug", [P, 2, TPB * HEADS * 32])
        junk = sb("junk", [P, 2, SEQ], BF16)

        s_x = [sem(f"x_loaded{i}") for i in range(X_LOADS)]
        s_w = sem("weights_loaded")
        s_wf0 = sem("ffn0_weights_loaded")
        s_wf1 = sem("ffn1_weights_loaded")
        s_zd = sem("sorted_x_zeroed")
        s_cst = sem("constants_ready")
        s_set_pe = sem("setup_pe")
        s_set_dv = sem("setup_dve")
        s_stat = sem("stats_step")
        s_sq = sem("sqrt_done")
        s_rt_dv = sem("routing_dve")
        s_rt_pe = sem("routing_pe")
        s_rt_ac = sem("routing_act")
        s_route = sem("routed")
        s_out = sem("out_stored")

        cB = [{n: count(f"{n}_l{l}") for n in ("b_xs", "b_T", "b_xT", "b_lg", "b_lgc")} for l in range(2)]
        cC = {n: count(n) for n in ("c_xs", "c_T", "c_xT", "c_qkv", "c_v", "c_qk", "c_proj", "c_exp", "c_kv",
                                    "c_kvm", "c_qz", "c_qzT", "c_qzTc", "c_kvo", "c_kvoc", "c_o", "c_x",
                                    "c_xr")}
        s_scat = [[count(f"scattered_l{l}_{u}", 16 * TPB, 0) for u in range(2)] for l in range(2)]
        cD = [{n: count(f"{n}_l{l}") for n in ("d_T", "d_xT", "d_h", "d_hs", "d_hT", "d_hb", "d_ha", "d_y",
                                               "d_ys")} for l in range(2)]
        s_xin = [[count(f"slots_in_l{l}_{u}", 16) for u in range(2)] for l in range(2)]
        s_yout = [[count(f"slots_out_l{l}_{u}", 16) for u in range(2)] for l in range(2)]
        s_gat = [[count(f"gathered_l{l}_{u}", 16 * TPB, 0) for u in range(2)] for l in range(2)]
        cG = [count(f"combined_l{l}") for l in range(2)]
        c_idx = [count(f"indices_l{l}") for l in range(2)]
        s_f1 = sem("ffn1_weights_folded")
        cF = {n: count(n, per) for n, per in (
            ("f_xs", 1), ("f_xadd", 1), ("f_xr", 1), ("f_A", 7), ("f_Ae", 5), ("f_va", 1), ("f_sq", 1), ("f_ms", 1),
            ("f_ln", 1), ("f_p1", 2), ("f_qn", 1), ("f_kn", 1), ("f_kn0", 1), ("f_kw", 1), ("f_r1", 2), ("f_p2", 1), ("f_p3", 1),
            ("f_S", 64), ("f_mx", 64), ("f_ST", 64), ("f_P", 64), ("f_PV", 64), ("f_O", 4), ("f_OT", 4),
            ("f_att", 4), ("f_fin", 1), ("f_mp", 2), ("f_mT", 2), ("f_mTc", 2))}
        s_parts = [count(f"parts_written{u}", 16) for u in range(2)]
        s_stack = [[count(f"stack_loaded{u}{h}", 16 * 4 * len(PARTS)) for h in range(2)] for u in range(2)]
        s_mrw = [count(f"mrow_written{h}", 16) for h in range(2)]
        s_mrl = [count(f"mrow_loaded{h}", 32) for h in range(2)]
        s_one = sem("ones_in_stacks")

        counts_by_engine = {
            "pe": [c[n] for c in cB for n in ("b_T", "b_lg")] + [cC[n] for n in ("c_T", "c_qkv", "c_proj", "c_kv",
                  "c_qzT", "c_kvo", "c_o")] + [c[n] for c in cD for n in ("d_T", "d_h", "d_hT", "d_y")]
                  + [cF[n] for n in ("f_A", "f_S", "f_ST", "f_PV", "f_OT", "f_mT")],
            "dve": [c[n] for c in cB for n in ("b_xs", "b_lgc")] + [cC[n] for n in ("c_xs", "c_v", "c_kvm", "c_qz",
                   "c_qzTc", "c_kvoc", "c_x")] + [c[n] for c in cD for n in ("d_hb", "d_ys")] + cG
                   + [cF[n] for n in ("f_xs", "f_ms", "f_qn", "f_kn0", "f_r1", "f_mx", "f_att", "f_mp")],
            "act": [c["b_xT"] for c in cB] + [cC[n] for n in ("c_xT", "c_qk", "c_exp")]
                   + [c[n] for c in cD for n in ("d_xT", "d_hs", "d_ha")]
                   + [cF[n] for n in ("f_Ae", "f_ln", "f_p1", "f_p2", "f_P", "f_O", "f_mTc")],
            "sp": [c for n in (s_xin, s_yout, s_stack) for pair in n for c in pair] + s_parts + s_mrw + s_mrl,
            "pool": [cC["c_xr"]] + c_idx + [cF[n] for n in ("f_xadd", "f_xr", "f_va", "f_sq", "f_kn", "f_kw", "f_p3", "f_fin")],
        }

        tiles_of = lambda k: bass.ds(k * TPB, TPB)
        v3 = lambda ap, n: ap.rearrange("p (t c) -> p t c", t=n)

        N_W = 16 * 25
        block = ctx.enter_context(nc.Block())

        @block.sync
        def _(sp):
            for c in counts_by_engine["sp"]:
                c.start(sp)
            small = [
                (wn[:, 0, :], Wq), (wn[:, 1, :], Wk), (wn[:, 2, :], Wv), (wn[:, 3, :], Wo),
                (vecs[:, 0:1], bq.unsqueeze(1)), (vecs[:, 1:2], bk.unsqueeze(1)), (vecs[:, 2:3], rms_w.unsqueeze(1)),
                (bvo[:, 0, :], bv.partition_broadcast(P)), (bvo[:, 1, :], bo.partition_broadcast(P)),
                (Rn[:, :], R), (gln[:, 0, :], gate_w), (gln[:, 1, :], centroids),
                (gb[0:E, :], gamma), (gb[E:2 * E, :], beta),
                (wsm[0:64, 0, 0:HD], W_DQ), (wsm[0:HD, 1, 0:64], W_UQ), (wsm[:, 2, 0:HD], W_DKV),
                (wsm[0:2 * HD, 3, :], W_UKV), (wsm[0:HD, 5, :], W_UKV[HD:2 * HD, :]),
                (wsm[0:64, 0, HD:2 * HD], W_QR), (wsm[0:64, 0, 2 * HD:3 * HD], W_KR), (wsm[0:HD, 4, 0:HD], W_O),
                (nrm8[:, 0:1], q_norm_w.unsqueeze(1)), (kwbc[:, :], k_norm_w.partition_broadcast(P)),
                (b1L[0][:, :], b1.rearrange("e (c f) -> (e c) f", c=FC)),
            ]
            assert 16 * len(small) == N_W
            xt = x.rearrange("b (t p) d -> p (b t) d", p=P)
            n_x = TILES // X_LOADS

            def load_x(i):
                sp.dma_start(X[:, i * n_x:(i + 1) * n_x, :], xt[:, i * n_x:(i + 1) * n_x, :]).then_inc(s_x[i], 16)
            load_x(0)
            for dst, src in small:
                sp.dma_start(dst, src).then_inc(s_w, 16)
            for i in range(1, X_LOADS):
                load_x(i)
            sp.wait_ge(s_cst, 1)
            zt = sorted_x.rearrange("(n p) d -> n p d", p=P)
            for n in range(SLOT_TILES // TPB):
                sp.dma_start(zt[n * TPB:(n + 1) * TPB].rearrange("t p d -> p t d"),
                             zeros512[:, :].rearrange("p (t d) -> p t d", t=TPB)).then_inc(s_zd, 16)
            for e in range(0, E, 2):
                sp.dma_start(W1s[:, e * F:(e + 2) * F].rearrange("p (e f) -> p e f", e=2),
                             W1[e:e + 2].rearrange("e d f -> d e f")).then_inc(s_wf0, 16)
                sp.dma_start(W2s[:, e * F:(e + 2) * F].rearrange("p (ec d) -> p ec d", ec=2 * FC),
                             W2[e:e + 2].rearrange("e (c p) d -> p (e c) d", p=P)).then_inc(s_wf0, 16)
            sp.dma_start(b2bc[:, :].rearrange("p (e d) -> p e d", e=E), b2.partition_broadcast(P)).then_inc(s_wf0, 16)

            def expert_io(l):
                for u in range(2):
                    sp.wait_ge(s_scat[l][u].handle, s_scat[l][u].at(BATCHES // 2 - 1, 64))

                def step(t, u, half, active):
                    if active[0]:
                        sp.wait_ge(cD[l]["d_T"].handle, cD[l]["d_T"].at(t - 2, 1))
                        sp.dma_start(xin[u], sorted_x[bass.ds(t * P, P), :]).then_inc(s_xin[l][u].handle, 16)
                    if active[5]:
                        w = (u + 1) % 2
                        sp.wait_ge(cD[l]["d_ys"].handle, cD[l]["d_ys"].at(t - 5, 1))
                        sp.dma_start(sorted_y[bass.ds((t - 5) * P, P), :], ys[w]).then_inc(s_yout[l][w].handle, 16)
                steps(sp, SLOT_TILES, 5, step)

            sp.wait_ge(cC["c_x"].handle, cC["c_x"].at(BATCHES - 1, 1))
            expert_io(0)
            sp.wait_ge(cD[0]["d_y"].handle, cD[0]["d_y"].at(SLOT_TILES - 1, 1))
            sp.wait_ge(cD[0]["d_ys"].handle, cD[0]["d_ys"].at(SLOT_TILES - 1, 1))
            for e in range(0, E, 2):
                sp.dma_start(W1s[:, e * F:(e + 2) * F].rearrange("p (e f) -> p e f", e=2),
                             w1[e:e + 2].rearrange("e d f -> d e f")).then_inc(s_wf1, 16)
                sp.dma_start(W2s[:, e * F:(e + 2) * F].rearrange("p (ec d) -> p ec d", ec=2 * FC),
                             w2[e:e + 2].rearrange("e (c p) d -> p (e c) d", p=P)).then_inc(s_wf1, 16)
            sp.dma_start(b2bc[:, :].rearrange("p (e d) -> p e d", e=E), fb2.partition_broadcast(P)).then_inc(s_wf1, 16)
            sp.dma_start(b1L[1][:, :], fb1.rearrange("e (c f) -> (e c) f", c=FC)).then_inc(s_wf1, 16)
            sp.wait_ge(s_one, 1)

            def attention_io(t, u, half, active):
                b, w = t - 1, (u + 1) % 2
                if active[0]:
                    sp.wait_ge(cF["f_p2"].handle, cF["f_p2"].at(t, 1))
                    sp.wait_ge(cF["f_p3"].handle, cF["f_p3"].at(t, 1))
                    for h in range(2):
                        sp.wait_ge(s_stack[u][h].handle, s_stack[u][h].at(half - 1, 384))
                    sp.dma_start(parts_d[u], parts[:, :, :]).then_inc(s_parts[u].handle, 16)
                    sp.wait_ge(s_parts[u].handle, s_parts[u].at(half, 16))

                def stack(h):
                    src = parts_d[u].rearrange("(pair par d) s t -> par s d pair t", par=2, d=HD)
                    for par in range(2):
                        for r, (pq, pk) in enumerate(PARTS):
                            rows = slice(64 * par + HD * r, 64 * par + HD * r + HD)
                            sp.dma_start(qst[u][rows, 4 * h:4 * h + 4, :], src[par][pq][:, 4 * h:4 * h + 4, :]) \
                                .then_inc(s_stack[u][h].handle, 16)
                            sp.dma_start(kst[u][rows, 4 * h:4 * h + 4, :], src[par][3 + pk][:, 4 * h:4 * h + 4, :]) \
                                .then_inc(s_stack[u][h].handle, 16)

                def mrows(k, w, h):
                    sp.wait_ge(cF["f_mTc"].handle, cF["f_mTc"].at(k, h + 1))
                    sp.wait_ge(s_mrl[h].handle, s_mrl[h].at(k - 1, 32))
                    sp.dma_start(mrow_d[h], mrowT[h][0:24, :]).then_inc(s_mrw[h].handle, 16)
                    sp.wait_ge(s_mrw[h].handle, s_mrw[h].at(k, 16))
                    src = mrow_d[h].rearrange("(s pair par) t -> par s pair t", pair=4, par=2)
                    for par in range(2):
                        rows = slice(64 * par + K_STACK, 64 * par + K_FULL)
                        sp.dma_start(qst[w][rows, 4 * h:4 * h + 4, :], src[par]).then_inc(s_mrl[h].handle, 16)

                if active[2]:
                    sp.wait_ge(cF["f_ST"].handle, cF["f_ST"].at(t - 2, 32))
                if active[0]:
                    stack(0)
                if active[1]:
                    mrows(b, w, 0)
                if active[2]:
                    sp.wait_ge(cF["f_ST"].handle, cF["f_ST"].at(t - 2, 64))
                if active[0]:
                    stack(1)
                if active[1]:
                    mrows(b, w, 1)
            steps(sp, BATCHES, 2, attention_io)

            sp.wait_ge(cF["f_fin"].handle, cF["f_fin"].at(BATCHES - 1, 1))
            expert_io(1)
            od = out.rearrange("b (t p) d -> p (b t) d", p=P)

            def store(t, u, half, active):
                sp.wait_ge(cG[1].handle, cG[1].at(t, 1))
                sp.dma_start(od[:, tiles_of(t), :], X[:, tiles_of(t), :]).then_inc(s_out, 16)
            steps(sp, BATCHES, 0, store)
            sp.wait_ge(s_out, 16 * BATCHES)

        @block.gpsimd
        def _(pool):
            for c in counts_by_engine["pool"]:
                c.start(pool)
            g = nc.gpsimd
            g.memset(zeros512[:, :], 0.0).then_inc(s_cst, 1)
            g.memset(ident[:, :], 0.0)
            g.memset(ones512[:, :], 1.0)
            g.memset(onesb[:, :], 1.0)
            g.memset(blk[:, :], 1.0)
            g.memset(maskS[:, :], 0.0)
            g.memset(rt[:, 0, 0:P], 0.0)
            g.memset(vaug[:, :, :], 0.0)
            g.iota(EID[:, :], pattern=[[1, SLOT_TILES]], base=0, channel_multiplier=0)
            g.iota(rs8i[:, :], pattern=[[-1, E]], base=E, channel_multiplier=0)
            pool.drain()
            g.tensor_copy(iotaJ[:, :], EID[:, :])
            g.tensor_copy(iotaE[:, :], rs8i[:, :])
            g.affine_select(out=ident[:, :], in_=ident[:, :], compare_op=ALU.not_equal, fill=1.0, base=0,
                            pattern=[[-1, P]], channel_multiplier=1)
            g.affine_select(out=tri[:, :], in_=onesb[:, :], compare_op=ALU.is_gt, fill=0.0, base=0,
                            pattern=[[1, P]], channel_multiplier=-1)
            g.affine_select(out=maskT[:, :], in_=rt[:, 0, 0:P], compare_op=ALU.is_ge, fill=LOW, base=0,
                            pattern=[[1, P]], channel_multiplier=-1)
            g.affine_select(out=maskS[:, SEQ - P:], in_=maskS[:, SEQ - P:], compare_op=ALU.is_ge, fill=LOW, base=0,
                            pattern=[[-1, P]], channel_multiplier=1)
            bv3 = blk[:, :].rearrange("p (h d) -> p h d", h=HEADS)
            g.affine_select(out=bv3, in_=bv3, compare_op=ALU.is_ge, fill=0.0, base=0,
                            pattern=[[-HD, HEADS], [0, HD]], channel_multiplier=1)
            pool.drain()
            g.affine_select(out=bv3, in_=bv3, compare_op=ALU.is_ge, fill=0.0, base=HD - 1,
                            pattern=[[HD, HEADS], [0, HD]], channel_multiplier=-1)
            for u in range(2):
                one_col = vaug[:, u, :].rearrange("p (th c) -> p th c", c=32)[:, :, HD:HD + 1]
                g.memset(one_col, 1.0)
            pool.drain()
            g.tensor_copy(identb[:, :], ident[:, :]).then_inc(s_cst, 1)

            def scatter(l, k, u, half):
                pool.nop(nofuse=True)
                for t in range(TPB):
                    g.indirect_dma_start(sorted_x[:, :], bass.IndirectOffsetOnAxis(ap=idx[:, u, t:t + 1], axis=0),
                                         xr[:, u, t * D:(t + 1) * D], None).then_inc(s_scat[l][u].handle, 16)

            def scaled_rows(k, u):
                g.tensor_tensor(v3(xr[:, u, :], TPB), v3(xs[:, u, :], TPB),
                                R2[:, tiles_of(k)].unsqueeze(2).to_broadcast([P, TPB, D]), ALU.mult)
                return g.tensor_copy(idx[:, u, :], POS[:, tiles_of(k)])

            pool.wait_ge(s_route, 1)
            pool.wait_ge(s_zd, 16 * (SLOT_TILES // TPB))

            def layer0(t, u, half, active):
                pool.wait_ge(cC["c_xs"].handle, cC["c_xs"].at(t, 1))
                pool.wait_ge(s_scat[0][u].handle, s_scat[0][u].at(half - 1, 64))
                scaled_rows(t, u).then_inc(cC["c_xr"].handle, 1)
                pool.wait_ge(cC["c_xr"].handle, cC["c_xr"].at(t, 1))
                scatter(0, t, u, half)
            steps(pool, BATCHES, 0, layer0, 2)

            def gather(l):
                for u in range(2):
                    pool.wait_ge(s_yout[l][u].handle, s_yout[l][u].at(SLOT_TILES // 2 - 1, 16))
                    pool.wait_ge(s_scat[l][u].handle, s_scat[l][u].at(BATCHES // 2 - 1, 64))

                def step(t, u, half, active):
                    pool.wait_ge(cG[l].handle, cG[l].at(t - 2, 1))
                    pool.wait_ge(s_gat[l][u].handle, s_gat[l][u].at(half - 1, 64))
                    pool.nop(nofuse=True)
                    g.tensor_copy(idx[:, u, :], POS[:, tiles_of(t)]).then_inc(c_idx[l].handle, 1)
                    pool.wait_ge(c_idx[l].handle, c_idx[l].at(t, 1))
                    pool.nop(nofuse=True)
                    for j in range(TPB):
                        g.indirect_dma_start(yg[:, u, j * D:(j + 1) * D], None, sorted_y[:, :],
                                             bass.IndirectOffsetOnAxis(ap=idx[:, u, j:j + 1], axis=0)) \
                            .then_inc(s_gat[l][u].handle, 16)
                steps(pool, BATCHES, 0, step, 2)
            gather(0)

            pool.wait_ge(cG[0].handle, cG[0].at(BATCHES - 1, 1))
            for u in range(2):
                g.memset(kst[u], 1.0)
                ins = g.memset(qst[u], 0.0)
            ins.then_inc(s_one, 1)
            pool.wait_ge(s_route, 2)
            for u in range(2):
                pool.wait_ge(s_gat[0][u].handle, s_gat[0][u].at(BATCHES // 2 - 1, 64))

            def layer1(t, u, half, active):
                if active[1]:
                    w = (u + 1) % 2
                    pool.wait_ge(cF["f_Ae"].handle, cF["f_Ae"].at(t - 1, 5))
                    pool.wait_ge(cF["f_PV"].handle, cF["f_PV"].at(t - 3, 64))
                    pool.nop(nofuse=True)
                    g.tensor_copy(vaug[:, w, :].rearrange("p (th r) -> p th r", r=32)[:, :, 0:HD],
                                  vst.rearrange("p t (h d) -> p (t h) d", d=HD)).then_inc(cF["f_va"].handle, 1)
                if active[0]:
                    pool.wait_ge(cF["f_xs"].handle, cF["f_xs"].at(t, 1))
                    pool.wait_ge(s_scat[1][u].handle, s_scat[1][u].at(half - 1, 64))
                    scaled_rows(t, u).then_inc(cF["f_xr"].handle, 1)
                    g.tensor_tensor(X[:, tiles_of(t), :], X[:, tiles_of(t), :], v3(xs[:, u, :], TPB),
                                    ALU.add).then_inc(cF["f_xadd"].handle, 1)
                    pool.wait_ge(cF["f_xr"].handle, cF["f_xr"].at(t, 1))
                    scatter(1, t, u, half)
                    pool.wait_ge(cF["f_Ae"].handle, cF["f_Ae"].at(t, 5))
                    pool.wait_ge(cF["f_ms"].handle, cF["f_ms"].at(t - 1, 1))
                    qk = raw[:, :, 0:256]
                    g.tensor_tensor(v3(sq, TPB), qk, qk, ALU.mult).then_inc(cF["f_sq"].handle, 1)
                    pool.wait_ge(cF["f_kn0"].handle, cF["f_kn0"].at(t, 1))
                    k3 = kn.rearrange("p (n d) -> p n d", d=HD)
                    g.tensor_tensor(k3, k3, kwbc[:, :].unsqueeze(1).to_broadcast([P, SEQ // HD, HD]),
                                    ALU.mult).then_inc(cF["f_kw"].handle, 1)
                    pool.wait_ge(cF["f_kw"].handle, cF["f_kw"].at(t, 1))
                    g.tensor_tensor(v3(kn, TPB), v3(kn, TPB), raw[:, :, 256:384], ALU.add) \
                        .then_inc(cF["f_kn"].handle, 1)
                    pool.wait_ge(cF["f_p2"].handle, cF["f_p2"].at(t, 1))
                    for a in range(2):
                        ins = g.tensor_tensor(parts[:, 3 * a + 2, :], r1[:, a, :], parts[:, 3 * a + 1, :],
                                              ALU.subtract)
                    ins.then_inc(cF["f_p3"].handle, 1)
                if active[2]:
                    pool.wait_ge(cF["f_att"].handle, cF["f_att"].at(t - 2, 4))
                    g.tensor_tensor(X[:, tiles_of(t - 2), :], X[:, tiles_of(t - 2), :], v3(att, TPB), ALU.add) \
                        .then_inc(cF["f_fin"].handle, 1)
            steps(pool, BATCHES, 2, layer1)
            gather(1)

        @block.vector
        def _(dve):
            for c in counts_by_engine["dve"]:
                c.start(dve)
            v = nc.vector
            dve_e = dve.alloc_register("dve_expert")

            def tt(out, a, b, op):
                return v.tensor_tensor(out, a, b, op)

            dve.wait_ge(s_cst, 2)
            dve.wait_ge(s_w, N_W)
            v.tensor_scalar(sqblk[:, :], blk[:, :], -0.5 / HD, None, ALU.mult).then_inc(s_set_dv, 1)
            dve.wait_ge(s_set_pe, 1)
            v.tensor_copy(wT[:, :, :].rearrange("p a b -> p (a b)"), bank[0][:, :])
            v.tensor_copy(glT[:, :, :].rearrange("p a b -> p (a b)"), bank[1][:, 0:2 * E])
            v.tensor_copy(gbT[:, :], bank[1][:, 16:16 + 2 * E])
            v.tensor_copy(b1T[:, :], bank[1][:, 32:32 + E * FC])
            rep = lambda src, n: src.unsqueeze(1).to_broadcast([n, HEADS, HD])
            r3 = lambda i, n: wrep[0:n, i, :].rearrange("p (h d) -> p h d", h=HEADS)
            v.tensor_copy(r3(0, 64), rep(wsm[0:64, 0, 0:HD], 64))
            v.tensor_copy(r3(1, 64), rep(bank[1][0:64, 64:64 + HD], 64))
            v.tensor_copy(r3(2, P), rep(wsm[:, 2, 0:HD], P))
            v.tensor_copy(r3(3, P), rep(bank[1][:, 72:72 + HD], P))
            v.tensor_copy(r3(4, 64), rep(wsm[0:64, 0, HD:2 * HD], 64))
            v.tensor_copy(r3(5, 64), rep(wsm[0:64, 0, 2 * HD:3 * HD], 64))
            v.tensor_copy(r3(6, HD), rep(bank[1][0:HD, 88:88 + HD], HD))
            v.tensor_copy(wsm[0:HD, 1, :].rearrange("p (h d) -> p h d", h=HEADS),
                          rep(ident[0:HD, 0:HD], HD)).then_inc(s_set_dv, 1)
            dve.wait_ge(s_set_pe, 2)
            v.tensor_copy(wrep[:, 7, :], bank[2][:, 0:P]).then_inc(s_set_dv, 1)
            rcol = bank[2][:, P:P + HD].unsqueeze(1).to_broadcast([P, HEADS, HD])
            b3 = lambda ap: ap.rearrange("p (h d) -> p h d", h=HEADS)
            tt(b3(Rblk[:, :]), rcol, b3(blk[:, :]), ALU.mult)
            v.tensor_scalar(vecs[:, 3:4], bank[2][:, 136:137], HD ** -0.5, None, ALU.mult)
            v.tensor_scalar(glT[:, 0, :], glT[:, 0, :], vecs[:, 2:3], None, ALU.mult)
            dve.drain()
            v.tensor_scalar(Rblk[:, :], Rblk[:, :], HD ** -0.5, None, ALU.mult)
            dve.wait_ge(s_set_pe, 3)
            for i in range(4):
                ins = tt(PROJ[:, i * P:(i + 1) * P], bank[3][:, i * P:(i + 1) * P], blk[:, :], ALU.mult)
            ins.then_inc(s_set_dv, 1)

            def stats_of_batch(k):
                for t in range(TPB):
                    v.bn_stats(st6[:, t, :], X[:, k * TPB + t, :])
                dve.drain()
                for t in range(TPB):
                    v.bn_aggr(mv4[:, t, :], st6[:, t, :])
                dve.drain()
                return v.tensor_copy(MV[:, tiles_of(k), :], mv4[:, :, :])

            n_sqrt = [0]

            def rsqrt64(dst, src):
                dve.drain()
                v.tensor_copy(tmp64[:, 0, :], src).then_inc(s_stat, 1)
                n_sqrt[0] += 1
                dve.wait_ge(s_sq, n_sqrt[0])
                v.reciprocal(dst, tmp64[:, 1, :])
                dve.drain()
                tt(tmp64[:, 2, :], dst, dst, ALU.mult)
                dve.drain()
                tt(tmp64[:, 2, :], tmp64[:, 2, :], src, ALU.mult)
                dve.drain()
                v.tensor_scalar(tmp64[:, 2, :], tmp64[:, 2, :], -0.5, 1.5, ALU.mult, ALU.add)
                dve.drain()
                tt(dst, dst, tmp64[:, 2, :], ALU.mult)
                dve.drain()

            def norms(eps2):
                dve.drain()
                v.tensor_scalar(tmp64[:, 3, :], MV[:, :, 1], LN_EPS, None, ALU.add)
                rsqrt64(RS[:, :], tmp64[:, 3, :])
                tt(tmp64[:, 3, :], RS[:, :], RS[:, :], ALU.mult)
                dve.drain()
                tt(tmp64[:, 3, :], tmp64[:, 3, :], MV[:, :, 1], ALU.mult)
                dve.drain()
                v.tensor_scalar(tmp64[:, 3, :], tmp64[:, 3, :], eps2, None, ALU.add)
                rsqrt64(R2[:, :], tmp64[:, 3, :])

            def normalize(k, u):
                over = lambda a: a.to_broadcast([P, TPB, D])
                tt(v3(xs[:, u, :], TPB), X[:, tiles_of(k), :], over(MV[:, tiles_of(k), 0:1]), ALU.subtract)
                dve.drain()
                return tt(v3(xs[:, u, :], TPB), v3(xs[:, u, :], TPB), over(RS[:, tiles_of(k)].unsqueeze(2)), ALU.mult)

            def logits(l):
                c = cB[l]

                def step(t, u, half, active):
                    if active[0]:
                        dve.wait_ge(c["b_T"].handle, c["b_T"].at(t - 2, 1))
                        normalize(t, u).then_inc(c["b_xs"].handle, 1)
                    if active[1]:
                        w = (u + 1) % 2
                        dve.wait_ge(c["b_lg"].handle, c["b_lg"].at(t - 1, 1))
                        v.tensor_copy(LG[:, tiles_of(t - 1), :],
                                      v3(bank[2 + w][:, 0:TPB * E], TPB)).then_inc(c["b_lgc"].handle, 1)
                steps(dve, BATCHES, 1, step)

            n_pe = [0]

            def route(l):
                dve.drain()
                if l == 0:
                    tt(LG[:, :, :], LG[:, :, :], R2[:, :].unsqueeze(2).to_broadcast([P, TILES, E]), ALU.mult)
                    dve.drain()
                m = tmp64[:, 0, :]
                v.tensor_reduce(m, LG[:, :, :], AX_X, ALU.max)
                dve.drain()
                bc = lambda a: a.unsqueeze(2).to_broadcast([P, TILES, E])
                t3 = lambda i: rt[:, i, :].rearrange("p (t e) -> p t e", e=E)
                tt(t3(0), LG[:, :, :], bc(m), ALU.is_ge)
                dve.drain()
                tt(t3(0), t3(0), iotaE[:, :].unsqueeze(1).to_broadcast([P, TILES, E]), ALU.mult)
                dve.drain()
                v.tensor_reduce(tmp64[:, 1, :], t3(0), AX_X, ALU.max)
                if l == 0:
                    tt(t3(1), LG[:, :, :], bc(m), ALU.subtract)
                    dve.drain()
                    v.tensor_copy(t3(2), t3(1)).then_inc(s_rt_dv, 1)
                else:
                    dve.drain()
                    v.tensor_copy(tmp64[:, 2, :], m).then_inc(s_rt_dv, 1)
                dve.drain()
                tt(ohE[:, :, :].rearrange("p e t -> p t e"), t3(0), bc(tmp64[:, 1, :]), ALU.is_equal) \
                    .then_inc(s_rt_dv, 1)
                dve.wait_ge(s_rt_ac, l + 1)
                if l == 0:
                    v.tensor_reduce(tmp64[:, 3, :], t3(2), AX_X, ALU.add)
                else:
                    v.tensor_scalar(tmp64[:, 3, :], tmp64[:, 2, :], 1.0, None, ALU.add)
                dve.drain()
                v.reciprocal(SC[:, :], tmp64[:, 3, :])
                dve.wait_ge(s_rt_pe, l + 1)
                cnt, rank = bank[0][:, :], bank[1][:, :]
                cum = rt[:, 1, :]
                v.tensor_tensor_scan(cum, ones512[:, :], cnt, 0.0, ALU.mult, ALU.add)
                dve.drain()
                cum3 = cum.rearrange("p (e t) -> p e t", e=E)
                v.tensor_copy(rs8[:, 0, :], cum3[:, :, TILES - 1])
                tt(rt[:, 2, :], cum, cnt, ALU.subtract)
                v.memset(rs8[:, 1, 0:1], 0.0)
                dve.drain()
                v.tensor_copy(rs8[:, 1, 1:E], rs8[:, 0, 0:E - 1])
                tt(rt[:, 2, :], rt[:, 2, :], rank, ALU.add)
                dve.drain()
                tt(rs8[:, 2, :], rs8[:, 0, :], rs8[:, 1, :], ALU.subtract)
                dve.drain()
                v.tensor_scalar(rs8[:, 2, :], rs8[:, 2, :], float(P - 1), None, ALU.add)
                dve.drain()
                v.tensor_copy(rs8i[:, :], rs8[:, 2, :])
                dve.drain()
                v.tensor_scalar(rs8i[:, :], rs8i[:, :], P.bit_length() - 1, None, ALU.arith_shift_right)
                dve.drain()
                v.tensor_copy(rs8[:, 3, :], rs8i[:, :])
                dve.drain()
                v.tensor_tensor_scan(rs8[:, 4, :], ones512[:, 0:E], rs8[:, 3, :], 0.0, ALU.mult, ALU.add)
                dve.drain()
                tt(rs8[:, 5, :], rs8[:, 4, :], rs8[:, 3, :], ALU.subtract)
                tt(rj[:, :, :], iotaJ[:, :].unsqueeze(2).to_broadcast([P, SLOT_TILES, E]),
                   rs8[:, 4, :].unsqueeze(1).to_broadcast([P, SLOT_TILES, E]), ALU.is_ge)
                dve.drain()
                v.tensor_reduce(rjs[:, :], rj[:, :, :], AX_X, ALU.add)
                v.tensor_scalar(rs8[:, 6, :], rs8[:, 5, :], float(P), None, ALU.mult)
                dve.drain()
                v.tensor_scalar(rjs[:, :], rjs[:, :], float(E - 1), None, ALU.min)
                tt(rs8[:, 7, :], rs8[:, 6, :], rs8[:, 1, :], ALU.subtract)
                dve.drain()
                v.tensor_copy(EID[:, :], rjs[:, :])
                e3 = lambda i: rt[:, i, :].rearrange("p (e t) -> p e t", e=E)
                tt(e3(2), e3(2), rs8[:, 7, :].unsqueeze(2).to_broadcast([P, E, TILES]), ALU.add)
                dve.drain()
                tt(e3(2), e3(2), ohE[:, :, :], ALU.mult)
                dve.drain()
                v.tensor_reduce(tmp64[:, 0, :], rt[:, 2, :].rearrange("p (e t) -> p t e", e=E), AX_X, ALU.add)
                dve.drain()
                v.tensor_copy(POS[:, :], tmp64[:, 0, :]).then_inc(s_route, 1)

            for i in range(X_LOADS):
                dve.wait_ge(s_x[i], 16)
                first = i * (BATCHES // X_LOADS)
                steps(dve, BATCHES // X_LOADS, 0, lambda t, u, half, active, first=first: stats_of_batch(t + first))
            norms(RMS_EPS0)
            logits(0)
            route(0)
            dve.wait_ge(s_wf0, 16 * 9)
            v.tensor_scalar(W1s[:, :], W1s[:, :], vecs[:, 2:3], None, ALU.mult)

            def attention0(t, u, half, active):
                c = cC
                w = (u + 1) % 2
                if active[0]:
                    dve.wait_ge(c["c_T"].handle, c["c_T"].at(t - 2, 1))
                    dve.wait_ge(c["c_xr"].handle, c["c_xr"].at(t - 2, 1))
                    normalize(t, u).then_inc(c["c_xs"].handle, 1)
                if active[1]:
                    dve.wait_ge(c["c_qkv"].handle, c["c_qkv"].at(t - 1, 1))
                    dve.wait_ge(c["c_kv"].handle, c["c_kv"].at(t - 3 + 0, 1))
                    tt(v3(v_s[w], TPB), v3(bank[3][:, :], TPB),
                       bvo[:, 0, :].unsqueeze(1).to_broadcast([P, TPB, D]), ALU.add).then_inc(c["c_v"].handle, 1)
                if active[2]:
                    k = t - 2
                    dve.wait_ge(c["c_exp"].handle, c["c_exp"].at(k, 1))
                    q3 = qp.rearrange("p (n d) -> p n d", d=HD)
                    v.tensor_reduce(qs, q3, AX_X, ALU.add)
                    dve.drain()
                    v.tensor_scalar(qs, qs, 1e-8, None, ALU.add)
                    dve.drain()
                    v.reciprocal(qr, qs)
                    dve.drain()
                    dve.wait_ge(c["c_qzT"].handle, c["c_qzT"].at(k - 1, 1))
                    tt(qz.rearrange("p (n d) -> p n d", d=HD), q3,
                       qr.unsqueeze(2).to_broadcast([P, TPB * HEADS, HD]), ALU.mult).then_inc(c["c_qz"].handle, 1)
                    dve.wait_ge(c["c_kv"].handle, c["c_kv"].at(k, 1))
                    tt(kvm, bank[7][:, 0:P], blk[:, :], ALU.mult).then_inc(c["c_kvm"].handle, 1)
                    dve.wait_ge(c["c_qzT"].handle, c["c_qzT"].at(k, 1))
                    v.tensor_copy(qzT, bank[6][:, :]).then_inc(c["c_qzTc"].handle, 1)
                    dve.wait_ge(c["c_kvo"].handle, c["c_kvo"].at(k, 1))
                    v.tensor_copy(kvo, bank[7][:, P:2 * P]).then_inc(c["c_kvoc"].handle, 1)
                    dve.wait_ge(c["c_o"].handle, c["c_o"].at(k, 1))
                    tt(v3(ot, TPB), v3(bank[0][:, :], TPB),
                       bvo[:, 1, :].unsqueeze(1).to_broadcast([P, TPB, D]), ALU.add)
                    dve.drain()
                    tt(X[:, tiles_of(k), :], X[:, tiles_of(k), :], v3(ot, TPB), ALU.add) \
                        .then_inc(c["c_x"].handle, 1)
            steps(dve, BATCHES, 2, attention0)

            def experts(l):
                c = cD[l]

                def step(t, u, half, active):
                    if active[2]:
                        k = t - 2
                        e = expert_of(dve, dve_e, EID, k)
                        dve.wait_ge(c["d_hT"].handle, c["d_hT"].at(k, 1))
                        dve.wait_ge(c["d_ha"].handle, c["d_ha"].at(k - 2, 1))
                        tt(v3(hb[u], FC), v3(bank[3 + u][:, :], FC),
                           b1T[:, bass.ds(e * FC, FC)].unsqueeze(2).to_broadcast([P, FC, P]), ALU.add) \
                            .then_inc(c["d_hb"].handle, 1)
                    if active[4]:
                        k = t - 4
                        e = expert_of(dve, dve_e, EID, k)
                        dve.wait_ge(c["d_y"].handle, c["d_y"].at(k, 1))
                        dve.wait_ge(s_yout[l][u].handle, s_yout[l][u].at(half - 3, 16))
                        tt(ys[u], bank[5 + u][:, 0:D], b2bc[:, bass.ds(e * D, D)], ALU.add) \
                            .then_inc(c["d_ys"].handle, 1)
                steps(dve, SLOT_TILES, 4, step)

            def combine(l, with_stats):
                def step(t, u, half, active):
                    dve.wait_ge(s_gat[l][u].handle, s_gat[l][u].at(half, 64))
                    if l == 1:
                        dve.wait_ge(cF["f_fin"].handle, cF["f_fin"].at(t, 1))
                    for j in range(TPB):
                        ins = v.scalar_tensor_tensor(out=X[:, t * TPB + j, :], in0=yg[:, u, j * D:(j + 1) * D],
                                                     scalar=SC[:, bass.ds(t * TPB + j, 1)], op0=ALU.mult,
                                                     in1=X[:, t * TPB + j, :], op1=ALU.add)
                    ins.then_inc(cG[l].handle, 1)
                    if with_stats:
                        dve.drain()
                        stats_of_batch(t)
                steps(dve, BATCHES, 0, step)

            experts(0)
            combine(0, True)

            norms(FFN_EPS1)
            logits(1)
            route(1)
            dve.wait_ge(s_wf1, 16 * 10)
            dve.wait_ge(s_set_pe, 4)
            v.tensor_copy(rt[:, 0, 0:E * FC], bank[1][:, 0:E * FC])
            dve.drain()
            tt(b1T[:, :], rt[:, 0, 0:E * FC], bank[2][:, 0:E * FC], ALU.add)
            for e in range(E):
                ins = v.tensor_scalar(W1s[:, e * F:(e + 1) * F], W1s[:, e * F:(e + 1) * F],
                                      gbT[:, e:e + 1], None, ALU.mult)
            ins.then_inc(s_f1, 1)

            s_items = [(h, qt) for h in range(HEADS) for qt in range(TPB)]

            def attention1(t, u, half, active):
                c = cF
                a, b, k = t, t - 1, t - 2
                w = (u + 1) % 2

                def at(name, i, n):
                    dve.wait_ge(c[name].handle, c[name].at(i, n))

                def maximum(n):
                    h, qt = s_items[n]
                    width = (qt + 1) * P
                    at("f_S", b, n + 1)
                    at("f_mx", b, n - 1)
                    dve.nop(nofuse=True)
                    v.tensor_tensor_reduce(out=junk[:, n % 2, 0:width], in0=bank[n % 2][:, 0:width],
                                           in1=maskS[:, SEQ - width:], scale=1.0, scalar=3 * LOW,
                                           op0=ALU.add, op1=ALU.max, accum_out=MX[:, qt * HEADS + h:qt * HEADS + h + 1]) \
                        .then_inc(c["f_mx"].handle, 1)

                def max_parts(h):
                    m3 = MX.rearrange("p (q h) -> p q h", q=TPB)[:, :, 8 * h:8 * h + 8]
                    r = [mr[:, 32 * i:32 * i + 32].rearrange("p (q h) -> p q h", q=TPB) for i in range(3)]
                    mp = mparts[:, 96 * h:96 * h + 96].rearrange("p (q s h) -> p q s h", q=TPB, s=3)
                    dve.drain()
                    v.tensor_scalar(r[0], m3, -1.0, None, ALU.mult)
                    dve.drain()
                    at("f_mT", b - 1, h + 1)
                    v.tensor_copy(mp[:, :, 0, :], r[0])
                    dve.drain()
                    tt(r[1], r[0], mp[:, :, 0, :], ALU.subtract)
                    dve.drain()
                    v.tensor_copy(mp[:, :, 1, :], r[1])
                    dve.drain()
                    tt(mp[:, :, 2, :], r[1], mp[:, :, 1, :], ALU.subtract).then_inc(c["f_mp"].handle, 1)

                def prepare(n):
                    if n == 0:
                        at("f_A", a - 2, 1)
                        at("f_xadd", a - 2, 1)
                        normalize(a, u).then_inc(c["f_xs"].handle, 1)
                    if n == 20:
                        at("f_sq", a, 1)
                        v.tensor_reduce(ms, sq.rearrange("p (n d) -> p n d", d=HD), AX_X, ALU.add)
                        dve.drain()
                        v.tensor_scalar(ms, ms, 1.0 / HD, RMS_EPS1, ALU.mult, ALU.add).then_inc(c["f_ms"].handle, 1)
                    if n == 26:
                        at("f_ln", a, 1)
                        tt(rt1, rq, rq, ALU.mult)
                        dve.drain()
                        tt(rt1, rt1, ms, ALU.mult)
                        dve.drain()
                        v.tensor_scalar(rt1, rt1, -0.5, 1.5, ALU.mult, ALU.add)
                        dve.drain()
                        tt(rq, rq, rt1, ALU.mult)
                        dve.drain()
                        at("f_A", a - 1, 7)
                        r4 = rq.rearrange("p (t a h) -> p a t h", t=TPB, a=2)
                        for i, dst in ((1, kn), (0, qn)):
                            src = raw[:, :, 128 * i:128 * i + 128].rearrange("p t (h d) -> p t h d", d=HD)
                            ins = tt(dst.rearrange("p (t h d) -> p t h d", t=TPB, d=HD), src,
                                     r4[:, i].unsqueeze(3).to_broadcast([P, TPB, HEADS, HD]), ALU.mult)
                            ins.then_inc(c["f_kn0" if i else "f_qn"].handle, 1)
                    if n in (40, 46):
                        i = 0 if n == 40 else 1
                        at("f_p1", a, i + 1)
                        at("f_p3", a - 1, 1)
                        src = bank[6][:, :]
                        if i == 0:
                            v.scalar_tensor_tensor(out=r1[:, 0, :], in0=src, scalar=vecs[:, 3:4], op0=ALU.mult,
                                                   in1=parts[:, 0, :], op1=ALU.subtract).then_inc(c["f_r1"].handle, 1)
                        else:
                            tt(r1[:, 1, :], src, parts[:, 3, :], ALU.subtract).then_inc(c["f_r1"].handle, 1)

                def normalized_output(qd):
                    at("f_OT", k, qd + 1)
                    o4 = bank[7][:, :].rearrange("p (t j r) -> p t j r", t=TPB, r=32)
                    v.reciprocal(rden.rearrange("p (t j) -> p t j", t=TPB), o4[:, :, :, HD])
                    dve.drain()
                    if qd == 0:
                        at("f_fin", k - 1, 1)
                    tt(att.rearrange("p (t g j d) -> p t g j d", t=TPB, g=QUADS, d=HD)[:, :, qd],
                       o4[:, :, :, 0:HD], rden.rearrange("p (t j) -> p t j", t=TPB).unsqueeze(3)
                       .to_broadcast([P, TPB, 4, HD]), ALU.mult).then_inc(c["f_att"].handle, 1)

                for n in range(64):
                    if active[0]:
                        prepare(n)
                    if active[1]:
                        maximum(n)
                        if n == 31:
                            max_parts(0)
                    if active[2] and n % 16 == 6 and n > 6:
                        normalized_output(n // 16 - 1)
                if active[1]:
                    max_parts(1)
                if active[2]:
                    normalized_output(3)
            steps(dve, BATCHES, 2, attention1)
            experts(1)
            combine(1, False)

        @block.scalar
        def _(act):
            for c in counts_by_engine["act"]:
                c.start(act)
            
            s = nc.scalar

            def root(n):
                act.wait_ge(s_stat, n)
                s.activation(tmp64[:, 1, :], tmp64[:, 0, :], ACT.Sqrt).then_inc(s_sq, 1)

            def transposed(l):
                c = cB[l]

                def step(t, u, half, active):
                    act.wait_ge(c["b_T"].handle, c["b_T"].at(t, 1))
                    act.wait_ge(c["b_lg"].handle, c["b_lg"].at(t - 2, 1))
                    s.copy(xT[:, u, :], bank[u][:, :]).then_inc(c["b_xT"].handle, 1)
                steps(act, BATCHES, 0, step)

            root(1)
            root(2)
            transposed(0)
            act.wait_ge(s_rt_dv, 1)
            s.activation(rt[:, 2, :], rt[:, 2, :], ACT.Exp).then_inc(s_rt_ac, 1)

            def attention0(t, u, half, active):
                c = cC
                if active[0]:
                    act.wait_ge(c["c_T"].handle, c["c_T"].at(t, 1))
                    act.wait_ge(c["c_qkv"].handle, c["c_qkv"].at(t - 1, 1))
                    s.copy(xT[:, 0, :], bank[0][:, :]).then_inc(c["c_xT"].handle, 1)
                    act.wait_ge(c["c_qkv"].handle, c["c_qkv"].at(t, 1))
                    act.wait_ge(c["c_proj"].handle, c["c_proj"].at(t - 1, 1))
                    s.activation(qT, bank[1][:, :], ACT.Identity, bias=vecs[:, 0:1])
                    s.activation(qsq, bank[1][:, :], ACT.Square, bias=vecs[:, 0:1])
                    s.activation(kT, bank[2][:, :], ACT.Identity, bias=vecs[:, 1:2])
                    s.activation(ksq, bank[2][:, :], ACT.Square, bias=vecs[:, 1:2]).then_inc(c["c_qk"].handle, 1)
                if active[1]:
                    k = t - 1
                    act.wait_ge(c["c_proj"].handle, c["c_proj"].at(k, 1))
                    act.wait_ge(c["c_kv"].handle, c["c_kv"].at(k - 1, 1))
                    act.wait_ge(c["c_qz"].handle, c["c_qz"].at(k - 1, 1))
                    s.activation(kp, bank[5][:, :], ACT.Exp)
                    s.activation(qp, bank[4][:, :], ACT.Exp).then_inc(c["c_exp"].handle, 1)
            steps(act, BATCHES, 1, attention0)

            def experts(l, func):
                c = cD[l]

                def step(t, u, half, active):
                    w = (u + 1) % 2
                    if active[0]:
                        act.wait_ge(c["d_T"].handle, c["d_T"].at(t, 1))
                        act.wait_ge(c["d_h"].handle, c["d_h"].at(t - 2, 1))
                        s.copy(xinT[u], bank[7 * u][:, 0:P]).then_inc(c["d_xT"].handle, 1)
                    if active[1]:
                        act.wait_ge(c["d_h"].handle, c["d_h"].at(t - 1, 1))
                        act.wait_ge(c["d_hT"].handle, c["d_hT"].at(t - 3, 1))
                        s.copy(hs[w], bank[1 + w][:, :]).then_inc(c["d_hs"].handle, 1)
                    if active[2]:
                        k = t - 2
                        act.wait_ge(c["d_hb"].handle, c["d_hb"].at(k, 1))
                        act.wait_ge(c["d_y"].handle, c["d_y"].at(k - 2, 1))
                        s.activation(ha[u], hb[u], func).then_inc(c["d_ha"].handle, 1)
                steps(act, SLOT_TILES, 2, step)
            experts(0, ACT.Silu)

            root(3)
            root(4)
            transposed(1)
            act.wait_ge(s_rt_dv, 3)
            s.activation(tmp64[:, 2, :], tmp64[:, 2, :], ACT.Exp, scale=-1.0).then_inc(s_rt_ac, 1)
            act.wait_ge(s_route, 2)

            def attention1(t, u, half, active):
                c = cF
                a, b, k = t, t - 1, t - 2
                w = (u + 1) % 2

                def at(name, i, n):
                    act.wait_ge(c[name].handle, c[name].at(i, n))

                def prepare(n):
                    if n == 1:
                        at("f_A", a, 1)
                        at("f_A", a - 1, 5)
                        s.copy(xT[:, 0, :], bank[6][:, :]).then_inc(c["f_Ae"].handle, 1)
                    if n in (4, 7, 10, 13):
                        j = (n - 4) // 3
                        at("f_A", a, j + 2)
                        if j == 0:
                            at("f_kn", a - 1, 1)
                            at("f_qn", a - 1, 1)
                            at("f_va", a - 1, 1)
                        s.copy(raw[:, j, :], bank[6][:, 0:384])
                        s.copy(vst[:, j, :], bank[6][:, 384:512]).then_inc(c["f_Ae"].handle, 1)
                    if n == 23:
                        at("f_ms", a, 1)
                        s.activation(rln, ms, ACT.Ln)
                        act.drain()
                        s.activation(rq, rln, ACT.Exp, scale=-0.5).then_inc(c["f_ln"].handle, 1)
                    if n in (39, 45):
                        i = 0 if n == 39 else 1
                        at("f_A", a, 6 + i)
                        if i == 0:
                            act.wait_ge(s_parts[w].handle, s_parts[w].at(half + u - 1, 16))
                            s.activation(parts[:, 0, :], bank[6][:, :], ACT.Identity, scale=vecs[:, 3:4]) \
                                .then_inc(cF["f_p1"].handle, 1)
                        else:
                            s.copy(parts[:, 3, :], bank[6][:, :]).then_inc(cF["f_p1"].handle, 1)
                    if n == 50:
                        at("f_r1", a, 2)
                        s.copy(parts[:, 1, :], r1[:, 0, :])
                        s.copy(parts[:, 4, :], r1[:, 1, :]).then_inc(c["f_p2"].handle, 1)

                def max_rows(h):
                    at("f_mT", b, h + 1)
                    act.wait_ge(s_mrw[h].handle, s_mrw[h].at(b - 1, 16))
                    s.copy(mrowT[h][0:24, :], bank[7][:, 0:256].bitcast(BF16)[0:24, :]) \
                        .then_inc(c["f_mTc"].handle, 1)

                for n in range(64):
                    if active[0]:
                        prepare(n)
                    if active[2]:
                        at("f_ST", k, n + 1)
                        at("f_PV", k, n - 3)
                        kt = (n % 8) // 2
                        s.activation(Pb[:, n % 4, 0:SEQ - kt * P], bank[2 + n % 2][:, 0:SEQ - kt * P], ACT.Exp) \
                            .then_inc(c["f_P"].handle, 1)
                        if n % 16 == 3 and n > 3:
                            evacuate_output(act, at, k, n // 16 - 1)
                    if active[1] and n == 35:
                        max_rows(0)
                if active[2]:
                    evacuate_output(act, at, k, 3)
                if active[1]:
                    max_rows(1)

            def evacuate_output(act, at, k, qd):
                at("f_PV", k, 16 * qd + 16)
                at("f_OT", k, qd)
                s.copy(OTs, bank[4 + qd % 2][:, :]).then_inc(cF["f_O"].handle, 1)
            steps(act, BATCHES, 2, attention1)
            experts(1, ACT.Relu)

        @block.tensor
        def _(pe):
            for c in counts_by_engine["pe"]:
                c.start(pe)
            mm = nc.tensor.matmul
            pe_e = [pe.alloc_register(f"pe_expert{i}") for i in range(2)]

            def product(out, lhsT, rhs, start=True, stop=True, skip=False):
                return mm(out, lhsT, rhs, start=start, stop=stop, skip_group_check=skip)

            def transpose(out, in_, n=P):
                return nc.tensor.transpose(out, in_, ident[0:n, 0:n])

            pe.wait_ge(s_cst, 2)
            pe.wait_ge(s_w, N_W)
            for i in range(4):
                transpose(bank[0][:, i * P:(i + 1) * P], wn[:, i, :])
            for i in range(2):
                transpose(bank[1][:, i * E:(i + 1) * E], gln[:, i, :], E)
            transpose(bank[1][:, 16:16 + 2 * E], gb[:, :], 2 * E)
            transpose(bank[1][:, 32:32 + E * FC], b1L[0][:, :], E * FC)
            transpose(bank[1][0:64, 64:64 + HD], wsm[0:HD, 1, 0:64], HD)
            transpose(bank[1][:, 72:72 + 2 * HD], wsm[0:2 * HD, 3, :], 2 * HD)
            transpose(bank[1][0:HD, 88:88 + HD], wsm[0:HD, 4, 0:HD], HD).then_inc(s_set_pe, 1)
            pe.wait_ge(s_set_dv, 2)
            product(bank[2][:, 0:P], wsm[0:HD, 5, :], wrep[0:HD, 6, :])
            product(bank[2][:, P:P + HD], wsm[0:HD, 1, :], Rn[:, :])
            product(bank[2][:, 136:137], wsm[0:HD, 1, :], nrm8[:, 0:1]).then_inc(s_set_pe, 1)
            pe.wait_ge(s_set_dv, 3)
            product(bank[3][:, P:2 * P], wrep[:, 2, :], wrep[:, 3, :])
            product(bank[3][:, 2 * P:3 * P], wrep[0:64, 5, :], wrep[0:64, 4, :])
            product(bank[3][:, 3 * P:4 * P], wrep[:, 2, :], wrep[:, 7, :])
            product(bank[3][:, 0:P], wrep[0:64, 0, :], wrep[0:64, 1, :]).then_inc(s_set_pe, 1)

            def logits(l):
                c = cB[l]

                def step(t, u, half, active):
                    if active[0]:
                        pe.wait_ge(c["b_xs"].handle, c["b_xs"].at(t, 1))
                        pe.wait_ge(c["b_xT"].handle, c["b_xT"].at(t - 2, 1))
                        for j in range(TPB):
                            ins = transpose(bank[u][:, j * P:(j + 1) * P], xs[:, u, j * D:(j + 1) * D])
                        ins.then_inc(c["b_T"].handle, 1)
                    if active[1]:
                        k, w = t - 1, (u + 1) % 2
                        pe.wait_ge(c["b_xT"].handle, c["b_xT"].at(k, 1))
                        pe.wait_ge(c["b_lgc"].handle, c["b_lgc"].at(k - 2, 1))
                        for j in range(TPB):
                            ins = product(bank[2 + w][:, j * E:(j + 1) * E], xT[:, w, j * P:(j + 1) * P], glT[:, l, :])
                        ins.then_inc(c["b_lg"].handle, 1)
                steps(pe, BATCHES, 1, step)

            def route(l):
                pe.wait_ge(s_rt_dv, 2 * l + 2)
                oh = ohE[:, :, :].rearrange("p e t -> p (e t)")
                product(bank[0][:, :], onesb[:, :], oh)
                product(bank[1][:, :], tri[:, :], oh).then_inc(s_rt_pe, 1)

            pe.wait_ge(s_set_dv, 4)
            logits(0)
            route(0)
            pe.wait_ge(s_route, 1)

            def attention0(t, u, half, active):
                c = cC
                if active[0]:
                    pe.wait_ge(c["c_xs"].handle, c["c_xs"].at(t, 1))
                    pe.wait_ge(c["c_x"].handle, c["c_x"].at(t - 3, 1))
                    for j in range(TPB):
                        ins = transpose(bank[0][:, j * P:(j + 1) * P], xs[:, u, j * D:(j + 1) * D])
                    ins.then_inc(c["c_T"].handle, 1)
                    pe.wait_ge(c["c_xT"].handle, c["c_xT"].at(t, 1))
                    pe.wait_ge(c["c_qk"].handle, c["c_qk"].at(t - 1, 1))
                    pe.wait_ge(c["c_v"].handle, c["c_v"].at(t - 1, 1))
                    product(bank[1][:, :], wT[:, 0, :], xT[:, 0, :])
                    product(bank[2][:, :], wT[:, 1, :], xT[:, 0, :])
                    for j in range(TPB):
                        ins = product(bank[3][:, j * P:(j + 1) * P], xT[:, 0, j * P:(j + 1) * P], wT[:, 2, :])
                    ins.then_inc(c["c_qkv"].handle, 1)
                if active[1]:
                    k = t - 1
                    pe.wait_ge(c["c_qk"].handle, c["c_qk"].at(k, 1))
                    pe.wait_ge(c["c_exp"].handle, c["c_exp"].at(k - 1, 1))
                    for bk_, a, b in ((4, qT, qsq), (5, kT, ksq)):
                        for j in range(TPB):
                            cols = slice(j * P, (j + 1) * P)
                            product(bank[bk_][:, cols], a[:, cols], Rblk[:, :], stop=False)
                            ins = product(bank[bk_][:, cols], b[:, cols], sqblk[:, :], start=False)
                    ins.then_inc(c["c_proj"].handle, 1)
                if active[2]:
                    k, w = t - 2, u
                    pe.wait_ge(c["c_exp"].handle, c["c_exp"].at(k, 1))
                    pe.wait_ge(c["c_v"].handle, c["c_v"].at(k, 1))
                    pe.wait_ge(c["c_kvoc"].handle, c["c_kvoc"].at(k - 1, 1))
                    for j in range(TPB):
                        cols = slice(j * P, (j + 1) * P)
                        ins = product(bank[7][:, 0:P], v_s[w][:, cols], kp[:, cols], start=(j == 0), stop=(j == TPB - 1))
                    ins.then_inc(c["c_kv"].handle, 1)
                    pe.wait_ge(c["c_qz"].handle, c["c_qz"].at(k, 1))
                    pe.wait_ge(c["c_qzTc"].handle, c["c_qzTc"].at(k - 1, 1))
                    for j in range(TPB):
                        ins = transpose(bank[6][:, j * P:(j + 1) * P], qz[:, j * P:(j + 1) * P])
                    ins.then_inc(c["c_qzT"].handle, 1)
                    pe.wait_ge(c["c_kvm"].handle, c["c_kvm"].at(k, 1))
                    product(bank[7][:, P:2 * P], kvm, wT[:, 3, :]).then_inc(c["c_kvo"].handle, 1)
                    pe.wait_ge(c["c_kvoc"].handle, c["c_kvoc"].at(k, 1))
                    pe.wait_ge(c["c_qzTc"].handle, c["c_qzTc"].at(k, 1))
                    if active[0]:
                        pe.wait_ge(c["c_xT"].handle, c["c_xT"].at(t, 1))
                    for j in range(TPB):
                        ins = product(bank[0][:, j * P:(j + 1) * P], qzT[:, j * P:(j + 1) * P], kvo)
                    ins.then_inc(c["c_o"].handle, 1)
            steps(pe, BATCHES, 2, attention0)

            def experts(l):
                c = cD[l]

                def step(t, u, half, active):
                    w = (u + 1) % 2
                    if active[0]:
                        pe.wait_ge(s_xin[l][u].handle, s_xin[l][u].at(half, 16))
                        pe.wait_ge(c["d_xT"].handle, c["d_xT"].at(t - 2, 1))
                        transpose(bank[7 * u][:, 0:P], xin[u]).then_inc(c["d_T"].handle, 1)
                    if active[4]:
                        k = t - 4
                        e = expert_of(pe, pe_e[1], EID, k)
                        pe.wait_ge(c["d_ha"].handle, c["d_ha"].at(k, 1))
                        pe.wait_ge(c["d_ys"].handle, c["d_ys"].at(k - 2, 1))
                        for j in range(FC):
                            ins = product(bank[5 + u][:, 0:D], ha[u][:, j * P:(j + 1) * P],
                                          W2s[:, bass.ds(e * (FC * D) + j * D, D)], start=(j == 0), stop=(j == FC - 1))
                        ins.then_inc(c["d_y"].handle, 1)
                    if active[1]:
                        k = t - 1
                        e = expert_of(pe, pe_e[0], EID, k)
                        pe.wait_ge(c["d_xT"].handle, c["d_xT"].at(k, 1))
                        pe.wait_ge(c["d_hs"].handle, c["d_hs"].at(k - 2, 1))
                        product(bank[1 + w][:, :], xinT[w], W1s[:, bass.ds(e * F, F)]).then_inc(c["d_h"].handle, 1)
                    if active[2]:
                        k = t - 2
                        pe.wait_ge(c["d_hs"].handle, c["d_hs"].at(k, 1))
                        pe.wait_ge(c["d_hb"].handle, c["d_hb"].at(k - 2, 1))
                        for j in range(FC):
                            ins = transpose(bank[3 + u][:, j * P:(j + 1) * P], hs[u][:, j * P:(j + 1) * P])
                        ins.then_inc(c["d_hT"].handle, 1)
                steps(pe, SLOT_TILES, 4, step)

            pe.wait_ge(cC["c_x"].handle, cC["c_x"].at(BATCHES - 1, 1))
            experts(0)

            logits(1)
            route(1)
            pe.wait_ge(s_route, 2)
            pe.wait_ge(s_wf1, 16 * 10)
            transpose(bank[1][:, 0:E * FC], b1L[1][:, :], E * FC)
            for e in range(E):
                for j in range(FC):
                    ins = product(bank[2][:, e * FC + j:e * FC + j + 1], W1s[:, e * F + j * P:e * F + (j + 1) * P],
                                  gbT[:, E + e:E + e + 1])
            ins.then_inc(s_set_pe, 1)
            pe.wait_ge(s_f1, 1)
            s_items = [(h, qt) for h in range(HEADS) for qt in range(TPB)]

            def attention1(t, u, half, active):
                c = cF
                a, b, k = t, t - 1, t - 2
                w = (u + 1) % 2

                def at(name, i, n):
                    pe.wait_ge(c[name].handle, c[name].at(i, n))

                def prepare(n):
                    if n == 0:
                        at("f_xs", a, 1)
                        at("f_r1", a - 1, 2)
                        for j in range(TPB):
                            ins = transpose(bank[6][:, j * P:(j + 1) * P], xs[:, u, j * D:(j + 1) * D])
                        ins.then_inc(c["f_A"].handle, 1)
                    if n in (3, 6, 9, 12):
                        j = n // 3 - 1
                        at("f_Ae", a, j + 1)
                        product(bank[6][:, :], xT[:, 0, j * P:(j + 1) * P], PROJ[:, :]).then_inc(c["f_A"].handle, 1)
                    if n in (38, 44):
                        if n == 38:
                            at("f_Ae", a, 5)
                            at("f_qn", a, 1)
                            src = qn
                        else:
                            at("f_kn", a, 1)
                            at("f_r1", a, 1)
                            src = kn
                        for j in range(TPB):
                            ins = transpose(bank[6][:, j * P:(j + 1) * P], src[:, j * P:(j + 1) * P])
                        ins.then_inc(c["f_A"].handle, 1)

                def score(n):
                    h, qt = s_items[n]
                    r = slice(64 * (h % 2), 64 * (h % 2) + K_STACK)
                    if n in (0, 32):
                        pe.wait_ge(s_stack[w][n // 32].handle, s_stack[w][n // 32].at(half + u - 1, 384))
                    at("f_mx", b, n - 1)
                    product(bank[n % 2][:, 0:(qt + 1) * P], qst[w][r, h // 2, qt * P:(qt + 1) * P],
                            kst[w][r, h // 2, 0:(qt + 1) * P]).then_inc(c["f_S"].handle, 1)

                def score_T(n):
                    pair, kt, par = n // 8, (n % 8) // 2, n % 2
                    r = slice(64 * par, 64 * par + K_FULL)
                    if n in (0, 32):
                        pe.wait_ge(s_mrl[n // 32].handle, s_mrl[n // 32].at(k, 32))
                    at("f_P", k, n - 1)
                    wide = SEQ - kt * P
                    product(bank[2 + par][:, 0:wide], kst[u][r, pair, kt * P:(kt + 1) * P],
                            qst[u][r, pair, kt * P:SEQ], stop=False)
                    product(bank[2 + par][:, 0:P], identb[:, :], maskT[:, :], start=False).then_inc(c["f_ST"].handle, 1)

                def values(n):
                    pair, kt, par = n // 8, (n % 8) // 2, n % 2
                    qd, j = pair // 2, 2 * (pair % 2) + par
                    h = 2 * pair + par
                    at("f_P", k, n + 1)
                    if n == 0:
                        at("f_va", k, 1)
                    if n % 16 == 0:
                        if qd >= 2:
                            at("f_O", k, qd - 1)
                        else:
                            at("f_O", k - 1, qd + 3)
                    va = vaug[:, u, (kt * HEADS + h) * 32:(kt * HEADS + h) * 32 + 32]
                    product(bank[4 + qd % 2][32 * j:32 * j + 32, kt * P:SEQ], va, Pb[:, n % 4, 0:SEQ - kt * P],
                            start=(kt == 0), stop=(kt == TPB - 1), skip=True).then_inc(c["f_PV"].handle, 1)

                def output_T(qd):
                    at("f_O", k, qd + 1)
                    at("f_att", k, qd)
                    if qd == 0:
                        at("f_mTc", k, 2)
                    elif active[1]:
                        at("f_mTc", b, 1)
                    for j in range(TPB):
                        ins = transpose(bank[7][:, j * P:(j + 1) * P], OTs[:, j * P:(j + 1) * P])
                    ins.then_inc(c["f_OT"].handle, 1)

                def max_rows(h):
                    at("f_mp", b, h + 1)
                    at("f_mTc", b - 1 + h, 2 - h)
                    if active[2]:
                        at("f_att", k, 1 if h == 0 else 4)
                    mp = mparts[:, 96 * h:96 * h + 96].rearrange("p (q s) -> p q s", q=TPB)
                    pb = bank[7][:, 0:256].bitcast(BF16)
                    for q in range(TPB):
                        ins = nc.tensor.transpose(pb[0:24, q * P:(q + 1) * P], mp[:, q, :], identb[:, :])
                    ins.then_inc(c["f_mT"].handle, 1)

                for n in range(64):
                    if active[0]:
                        prepare(n)
                    if active[1]:
                        score(n)
                    if active[2]:
                        score_T(n)
                        if n >= 2:
                            values(n - 2)
                        if n % 16 == 5 and n > 5:
                            output_T(n // 16 - 1)
                    if active[1] and n == 34:
                        max_rows(0)
                if active[2]:
                    values(62)
                    values(63)
                    output_T(3)
                if active[1]:
                    max_rows(1)

            steps(pe, BATCHES, 2, attention1)
            pe.wait_ge(cF["f_att"].handle, cF["f_att"].at(BATCHES - 1, 4))
            experts(1)


_INS = ['L0_attn_x', 'L0_attn_Wq', 'L0_attn_bq', 'L0_attn_Wk', 'L0_attn_bk', 'L0_attn_Wv', 'L0_attn_bv', 'L0_attn_Wo',
        'L0_attn_bo', 'L0_attn_R', 'L0_ffn_rms_w', 'L0_ffn_gate_w', 'L0_ffn_W1', 'L0_ffn_b1', 'L0_ffn_W2', 'L0_ffn_b2',
        'L1_attn_W_DQ', 'L1_attn_W_UQ', 'L1_attn_W_DKV', 'L1_attn_W_UKV', 'L1_attn_W_QR', 'L1_attn_W_KR', 'L1_attn_W_O',
        'L1_attn_q_norm_w', 'L1_attn_k_norm_w', 'L1_ffn_centroids', 'L1_ffn_w1', 'L1_ffn_b1', 'L1_ffn_w2', 'L1_ffn_b2',
        'L1_ffn_gamma', 'L1_ffn_beta']


def kernel(**inputs):
    from concourse import bacc
    from concourse.bass_utils import run_bass_kernel_spmd

    nc = bacc.Bacc("TRN2", target_bir_lowering=False, num_devices=1)
    nc.disable_value_cache = True
    arrays, args = {}, []
    for name in _INS:
        a = np.ascontiguousarray(inputs[name])
        arrays[f"in_{name}"] = a
        args.append(nc.dram_tensor(f"in_{name}", a.shape, mybir.dt.from_np(a.dtype), kind="ExternalInput").ap())
    args.append(nc.dram_tensor("out_x", (BATCHES, SEQ, D), F32, kind="ExternalOutput").ap())
    build(nc, *args)
    r = run_bass_kernel_spmd(nc, [arrays], core_ids=[0])
    return r.results[0]["out_x"]
```

```python
from contextlib import ExitStack

import numpy as np

import concourse.bass as bass
from concourse import mybir

F32 = mybir.dt.float32
BF16 = mybir.dt.bfloat16
I32 = mybir.dt.int32
ALU = mybir.AluOpType
ACT = mybir.ActivationFunctionType
AX_X = mybir.AxisListType.X

P = 128
D = 128
SEQ = 512
BATCHES = 16
TPB = SEQ // P
TILES = BATCHES * TPB
HEADS = 16
HD = D // HEADS
PAIRS = HEADS // 2
QUADS = HEADS // 4
E = 8
F = 512
FC = F // P
SLOT_TILES = TILES + E
PAIR_STEPS = SLOT_TILES // 2
HEAD = 2
X_LOADS = 4
RSQRT_GUESS = float(0x5F3759DF)
LOW = -1e30
PARTS = [(0, 0), (1, 0), (2, 0), (0, 1), (1, 1), (0, 2)]
PART_ROWS = [(0, 3, 0), (3, 2, 1), (5, 1, 2)]
K_STACK = len(PARTS) * HD
K_FULL = K_STACK + 3
ARENA = 17200
LN_EPS = 1e-5
RMS_EPS0 = 1e-6
RMS_EPS1 = 1.1920929e-07
FFN_EPS1 = 1e-5


def expert_of(eng, reg, table, tile):
    eng.reg_load(reg, table[0:1, bass.ds(tile, 1)])
    return eng.snap(reg, min_val=0, max_val=E - 1)


class Count:

    def __init__(self, handle, per, head=HEAD):
        self.handle, self.per, self.head = handle, per, head

    def at(self, k, c):
        return k * self.per + (self.per * self.head + c)

    def start(self, eng):
        eng.sem_inc(self.handle, self.per * self.head)


def steps(eng, items, depth, body, peel=0):
    begin = max(depth + depth % 2, peel)
    turns = (items - begin) // 2
    flags = lambda t: [0 <= t - s < items for s in range(depth + 1)]
    for t in range(begin):
        body(t, t % 2, t // 2, flags(t))
    if turns == 1:
        for u in range(2):
            body(begin + u, u, begin // 2, flags(begin + u))
    elif turns > 1:
        with eng.Fori(0, turns) as turn:
            for u in range(2):
                body(turn * 2 + (begin + u), u, turn + begin // 2, [True] * (depth + 1))
    for t in range(begin + 2 * turns, items + depth):
        body(t, t % 2, t // 2, flags(t))


def build(nc, x, Wq, bq, Wk, bk, Wv, bv, Wo, bo, R, rms_w, gate_w, W1, b1, W2, b2,
          W_DQ, W_UQ, W_DKV, W_UKV, W_QR, W_KR, W_O, q_norm_w, k_norm_w,
          centroids, w1, fb1, w2, fb2, gamma, beta, out):
    ctx = ExitStack()
    with ctx:
        def sb(name, shape, dt=F32):
            return ctx.enter_context(nc.sbuf_tensor(name, shape, dt))

        def sem(name):
            return ctx.enter_context(nc.semaphore(name))

        def count(name, per=1, head=HEAD):
            return Count(sem(name), per, head)

        bank = [ctx.enter_context(nc.psum_tensor(f"bank{i}", [P, 512], F32)) for i in range(8)]

        sorted_x = nc.dram_tensor("sorted_x", (SLOT_TILES * P, D), F32, kind="Internal").ap()
        sorted_y = nc.dram_tensor("sorted_y", (SLOT_TILES * P, D), F32, kind="Internal").ap()
        parts_d = [nc.dram_tensor(f"parts_d{u}", (6, 2, HD, PAIRS, SEQ), BF16, kind="Internal").ap() for u in range(2)]
        mrow_d = [nc.dram_tensor(f"mrow_d{h}", (24, SEQ), BF16, kind="Internal").ap() for h in range(2)]

        X = sb("X", [P, TILES, D])
        W1s = sb("W1s", [P, E * F])
        W2s = sb("W2s", [P, E * FC * D])
        b1T = sb("b1T", [P, E * FC])
        b1L = [sb(f"b1L{l}", [E * FC, P]) for l in range(2)]
        b2bc = sb("b2bc", [P, E * D])
        ident = sb("ident", [P, P])
        identb = sb("identb", [P, P], BF16)
        tri = sb("tri", [P, P], BF16)
        onesb = sb("onesb", [P, P], BF16)
        blk = sb("blk", [P, P])
        sqblk = sb("sqblk", [P, P])
        maskT = sb("maskT", [P, P], BF16)
        maskS = sb("maskS", [P, SEQ])
        ones512 = sb("ones512", [P, 512])
        zeros512 = sb("zeros512", [P, 512])
        iotaE = sb("iotaE", [P, E])
        iotaJ = sb("iotaJ", [P, SLOT_TILES])
        wn = sb("wn", [P, 4, P])
        wT = sb("wT", [P, 4, P])
        vecs = sb("vecs", [P, 8])
        bvo = sb("bvo", [P, 2, D])
        Rn = sb("Rn", [HD, HD])
        Rblk = sb("Rblk", [P, P])
        gln = sb("gln", [E, 2, D])
        glT = sb("glT", [P, 2, E])
        gb = sb("gb", [2 * E, D])
        gbT = sb("gbT", [P, 2 * E])
        Pb = sb("Pb", [P, 4, SEQ])
        setup_space = Pb[:, :, :].rearrange("p a n -> p (a n)")
        wsm = setup_space[:, 0:6 * P].rearrange("p (a n) -> p a n", n=P)
        wrep = setup_space[:, 6 * P:14 * P].rearrange("p (a n) -> p a n", n=P)
        PROJ = sb("PROJ", [P, 4 * P])
        nrm8 = sb("nrm8", [HD, 2])
        kwbc = sb("kwbc", [P, HD])
        MV = sb("MV", [P, TILES, 2])
        RS = sb("RS", [P, TILES])
        R2 = sb("R2", [P, TILES])
        tmp64 = sb("tmp64", [P, 4, TILES])
        LG = sb("LG", [P, TILES, E])
        ohE = sb("ohE", [P, E, TILES], BF16)
        rt = sb("rt", [P, 3, E * TILES])
        rsi = sb("rsi", [P, TILES], I32)
        rs8 = sb("rs8", [P, 8, E])
        rs8i = sb("rs8i", [P, E], I32)
        rj = sb("rj", [P, SLOT_TILES, E])
        rjs = sb("rjs", [P, SLOT_TILES])
        EID = sb("EID", [P, SLOT_TILES], I32)
        POS = sb("POS", [P, TILES], I32)
        SC = sb("SC", [P, TILES])
        xs = sb("xs", [P, 2, TPB * D])
        xr = sb("xr", [P, 2, TPB * D])
        idx = sb("idx", [P, 2, TPB], I32)
        xT = sb("xT", [P, 2, SEQ])
        st6 = sb("st6", [P, TPB, 6])
        mv4 = sb("mv4", [P, TPB, 2])
        yg = xr
        arena = sb("arena", [P, ARENA])
        at_ = [0]

        def carve(n, dt=F32):
            a = at_[0]
            at_[0] += n
            assert at_[0] <= ARENA, at_[0]
            v = arena[:, a:a + n]
            return v if dt == F32 else v.bitcast(dt)

        qT = carve(SEQ); kT = carve(SEQ); qsq = carve(SEQ); ksq = carve(SEQ)
        v_s = [carve(SEQ) for _ in range(2)]
        qp = carve(SEQ); kp = carve(SEQ)
        qz = carve(SEQ); qzT = carve(SEQ)
        qs = carve(TPB * HEADS); qr = carve(TPB * HEADS)
        kvm = carve(P); kvo = carve(P); ot = carve(SEQ)
        at_[0] = 0
        xin = [carve(2 * D) for _ in range(2)]
        xinT = [carve(2 * P) for _ in range(2)]
        w1e = [carve(2 * F) for _ in range(2)]
        hb = [carve(2 * F) for _ in range(2)]
        ha = [carve(2 * F) for _ in range(2)]
        ys = [carve(2 * D) for _ in range(2)]
        at_[0] = 0
        raw = carve(TPB * 4 * D).rearrange("p (t c) -> p t c", t=TPB)
        vst = raw[:, :, 3 * D:4 * D]
        sq = carve(TPB * 256)
        ms = carve(P); rq = carve(P); rt1 = carve(P); rgi = carve(P, I32)
        qn = carve(SEQ); kn = carve(SEQ)
        r1 = carve(2 * SEQ).rearrange("p (a n) -> p a n", a=2)
        parts = carve(6 * SEQ // 2, BF16).rearrange("p (a n) -> p a n", a=6)
        qst = [carve(PAIRS * SEQ // 2, BF16).rearrange("p (a n) -> p a n", a=PAIRS) for _ in range(2)]
        kst = [carve(PAIRS * SEQ // 2, BF16).rearrange("p (a n) -> p a n", a=PAIRS) for _ in range(2)]
        mrowT = [carve(SEQ // 2, BF16) for _ in range(2)]
        MX = carve(HEADS * TPB)
        mr = carve(3 * 32)
        att = carve(SEQ)
        OTs = carve(SEQ)
        rden = carve(HEADS)
        mparts = carve(2 * 3 * 8 * TPB // 2, BF16)
        vaug = sb("vaug", [P, 2, TPB * HEADS * 32])
        junk = sb("junk", [P, 2, SEQ], BF16)

        s_x = [sem(f"x_loaded{i}") for i in range(X_LOADS)]
        s_w = sem("weights_loaded")
        s_wf0 = sem("ffn0_weights_loaded")
        s_wf1 = sem("ffn1_weights_loaded")
        s_zd = sem("sorted_x_zeroed")
        s_cst = sem("constants_ready")
        s_set_pe = sem("setup_pe")
        s_set_dv = sem("setup_dve")
        s_rt_dv = sem("routing_dve")
        s_rt_pe = sem("routing_pe")
        s_rt_ac = sem("routing_act")
        s_route = sem("routed")
        s_out = sem("out_stored")

        cB = [{n: count(f"{n}_l{l}") for n in ("b_xs", "b_T", "b_xT", "b_lg", "b_lgc")} for l in range(2)]
        cC = {n: count(n) for n in ("c_xs", "c_T", "c_xT", "c_qkv", "c_v", "c_qk", "c_proj", "c_exp", "c_kv",
                                    "c_kvm", "c_or", "c_qz", "c_qzT", "c_qzTc", "c_kvo", "c_kvoc", "c_o", "c_x",
                                    "c_xr")}
        s_scat = [[count(f"scattered_l{l}_{u}", 16 * TPB, 0) for u in range(2)] for l in range(2)]
        cD = [{n: count(f"{n}_l{l}", 2 if n in ("d_h", "d_hb") else 1) for n in ("d_w", "d_wo", "d_T", "d_xT", "d_h", "d_hb", "d_ha", "d_y",
                                               "d_ys")} for l in range(2)]
        s_xin = [[count(f"slots_in_l{l}_{u}", 16) for u in range(2)] for l in range(2)]
        s_yout = [[count(f"slots_out_l{l}_{u}", 16) for u in range(2)] for l in range(2)]
        s_gat = [[count(f"gathered_l{l}_{u}", 16 * TPB, 0) for u in range(2)] for l in range(2)]
        c_stat = count("statistics_l0")
        s_gsum = sem("gate_sums")
        cG = [count(f"combined_l{l}") for l in range(2)]
        c_idx = [count(f"indices_l{l}") for l in range(2)]
        s_f1 = sem("ffn1_biases_folded")
        s_g0 = sem("ffn0_weights_scaled")
        s_g1 = sem("ffn1_weights_scaled")
        cF = {n: count(n, per) for n, per in (
            ("f_xs", 1), ("f_xc", 1), ("f_xadd", 1), ("f_xr", 1), ("f_A", 7), ("f_Ae", 5), ("f_va", 1), ("f_sq", 2), ("f_ms", 3), ("f_nw", 12),
            ("f_p1", 2), ("f_qn", 1), ("f_kn", 1), ("f_kn0", 1), ("f_kw", 1), ("f_r1", 2), ("f_p2", 2), ("f_p3", 2),
            ("f_S", 64), ("f_mx", 64), ("f_ST", 64), ("f_P", 64), ("f_PV", 64), ("f_O", 4), ("f_OT", 4),
            ("f_att", 4), ("f_fin", 1), ("f_mp", 2), ("f_mT", 2), ("f_mTc", 2))}
        s_parts = [count(f"parts_written{u}", 16 * PAIRS) for u in range(2)]
        s_stack = [[count(f"stack_loaded{u}{h}", 16 * 4 * len(PART_ROWS)) for h in range(2)] for u in range(2)]
        s_mrw = [count(f"mrow_written{h}", 16) for h in range(2)]
        s_mrl = [count(f"mrow_loaded{h}", 32) for h in range(2)]
        s_one = sem("ones_in_stacks")

        counts_by_engine = {
            "pe": [c[n] for c in cB for n in ("b_T", "b_lg")] + [cC[n] for n in ("c_T", "c_qkv", "c_proj", "c_kv",
                  "c_qzT", "c_kvo", "c_o")] + [c[n] for c in cD for n in ("d_T", "d_h", "d_y")]
                  + [cF[n] for n in ("f_A", "f_S", "f_ST", "f_PV", "f_OT", "f_mT")],
            "dve": [c_stat] + [cC[n] for n in ("c_xs", "c_v", "c_kvm", "c_qz",
                   "c_qzTc", "c_kvoc", "c_or", "c_x")] + [c[n] for c in cD for n in ("d_hb", "d_ys")] + cG
                   + [cF[n] for n in ("f_ms", "f_qn", "f_kn0", "f_r1", "f_mx", "f_att", "f_mp")],
            "act": [c[n] for c in cB for n in ("b_xs", "b_xT", "b_lgc")] + [cC[n] for n in ("c_xT", "c_qk", "c_exp")]
                   + [c[n] for c in cD for n in ("d_wo", "d_xT", "d_ha")]
                   + [cF[n] for n in ("f_Ae", "f_p1", "f_p2", "f_P", "f_O", "f_mTc")] + s_mrw + s_mrl,
            "sp": [c for n in (s_xin, s_yout, s_stack) for pair in n for c in pair] + s_parts,
            "pool": [cC["c_xr"]] + [c["d_w"] for c in cD] + c_idx + [cF[n] for n in ("f_xs", "f_xc", "f_xadd", "f_xr", "f_va", "f_sq", "f_nw", "f_kn", "f_kw", "f_p3", "f_fin")],
        }

        tiles_of = lambda k: bass.ds(k * TPB, TPB)
        v3 = lambda ap, n: ap.rearrange("p (t c) -> p t c", t=n)

        N_W = 16 * 25
        block = ctx.enter_context(nc.Block())

        @block.sync
        def _(sp):
            for c in counts_by_engine["sp"]:
                c.start(sp)
            small = [
                (wn[:, 0, :], Wq), (wn[:, 1, :], Wk), (wn[:, 2, :], Wv), (wn[:, 3, :], Wo),
                (vecs[:, 0:1], bq.unsqueeze(1)), (vecs[:, 1:2], bk.unsqueeze(1)), (vecs[:, 2:3], rms_w.unsqueeze(1)),
                (bvo[:, 0, :], bv.partition_broadcast(P)), (bvo[:, 1, :], bo.partition_broadcast(P)),
                (Rn[:, :], R), (gln[:, 0, :], gate_w), (gln[:, 1, :], centroids),
                (gb[0:E, :], gamma), (gb[E:2 * E, :], beta),
                (wsm[0:64, 0, 0:HD], W_DQ), (wsm[0:HD, 1, 0:64], W_UQ), (wsm[:, 2, 0:HD], W_DKV),
                (wsm[0:2 * HD, 3, :], W_UKV), (wsm[0:HD, 5, :], W_UKV[HD:2 * HD, :]),
                (wsm[0:64, 0, HD:2 * HD], W_QR), (wsm[0:64, 0, 2 * HD:3 * HD], W_KR), (wsm[0:HD, 4, 0:HD], W_O),
                (nrm8[:, 0:1], q_norm_w.unsqueeze(1)), (kwbc[:, :], k_norm_w.partition_broadcast(P)),
                (b1L[0][:, :], b1.rearrange("e (c f) -> (e c) f", c=FC)),
            ]
            assert 16 * len(small) == N_W
            xt = x.rearrange("b (t p) d -> p (b t) d", p=P)
            n_x = TILES // X_LOADS

            def load_x(i):
                sp.dma_start(X[:, i * n_x:(i + 1) * n_x, :], xt[:, i * n_x:(i + 1) * n_x, :]).then_inc(s_x[i], 16)
            load_x(0)
            for dst, src in small:
                sp.dma_start(dst, src).then_inc(s_w, 16)
            for i in range(1, X_LOADS):
                load_x(i)
            sp.wait_ge(s_cst, 1)
            zt = sorted_x.rearrange("(n p) d -> n p d", p=P)
            for n in range(SLOT_TILES // TPB):
                sp.dma_start(zt[n * TPB:(n + 1) * TPB].rearrange("t p d -> p t d"),
                             zeros512[:, :].rearrange("p (t d) -> p t d", t=TPB)).then_inc(s_zd, 16)
            for e in range(0, E, 2):
                sp.dma_start(W1s[:, e * F:(e + 2) * F].rearrange("p (e f) -> p e f", e=2),
                             W1[e:e + 2].rearrange("e d f -> d e f")).then_inc(s_wf0, 16)
                sp.dma_start(W2s[:, e * F:(e + 2) * F].rearrange("p (ec d) -> p ec d", ec=2 * FC),
                             W2[e:e + 2].rearrange("e (c p) d -> p (e c) d", p=P)).then_inc(s_wf0, 16)
            sp.dma_start(b2bc[:, :].rearrange("p (e d) -> p e d", e=E), b2.partition_broadcast(P)).then_inc(s_wf0, 16)

            def expert_io(l):
                for u in range(2):
                    sp.wait_ge(s_scat[l][u].handle, s_scat[l][u].at(BATCHES // 2 - 1, 64))

                rows = lambda d, k: d[bass.ds(k * (2 * P), 2 * P), :].rearrange("(i p) d -> p i d", p=P)

                def step(t, u, half, active):
                    if active[0]:
                        sp.wait_ge(cD[l]["d_T"].handle, cD[l]["d_T"].at(t - 2, 1))
                        sp.dma_start(v3(xin[u], 2), rows(sorted_x, t)).then_inc(s_xin[l][u].handle, 16)
                    if active[4]:
                        sp.wait_ge(cD[l]["d_ys"].handle, cD[l]["d_ys"].at(t - 4, 1))
                        sp.dma_start(rows(sorted_y, t - 4), v3(ys[u], 2)).then_inc(s_yout[l][u].handle, 16)
                steps(sp, PAIR_STEPS, 4, step)

            sp.wait_ge(cC["c_x"].handle, cC["c_x"].at(BATCHES - 1, 1))
            expert_io(0)
            sp.wait_ge(cD[0]["d_y"].handle, cD[0]["d_y"].at(PAIR_STEPS - 1, 1))
            sp.wait_ge(cD[0]["d_ys"].handle, cD[0]["d_ys"].at(PAIR_STEPS - 1, 1))
            for e in range(0, E, 2):
                sp.wait_ge(cG[0].handle, cG[0].at(e, 1))
                sp.dma_start(W1s[:, e * F:(e + 2) * F].rearrange("p (e f) -> p e f", e=2),
                             w1[e:e + 2].rearrange("e d f -> d e f")).then_inc(s_wf1, 16)
                sp.dma_start(W2s[:, e * F:(e + 2) * F].rearrange("p (ec d) -> p ec d", ec=2 * FC),
                             w2[e:e + 2].rearrange("e (c p) d -> p (e c) d", p=P)).then_inc(s_wf1, 16)
            sp.dma_start(b2bc[:, :].rearrange("p (e d) -> p e d", e=E), fb2.partition_broadcast(P)).then_inc(s_wf1, 16)
            sp.dma_start(b1L[1][:, :], fb1.rearrange("e (c f) -> (e c) f", c=FC)).then_inc(s_wf1, 16)
            sp.wait_ge(s_one, 1)

            def attention_io(t, u, half, active):
                def stack(h):
                    pairs = slice(4 * h, 4 * h + 4)
                    for par in range(2):
                        for first, n, pk in PART_ROWS:
                            rows = slice(64 * par + HD * first, 64 * par + HD * (first + n))
                            sp.dma_start(qst[u][rows, pairs, :], parts_d[u][0:n, par, :, pairs, :]) \
                                .then_inc(s_stack[u][h].handle, 16)
                            sp.dma_start(kst[u][rows, pairs, :], parts_d[u][3 + pk:4 + pk, par, :, pairs, :]
                                         .to_broadcast([n, HD, 4, SEQ])).then_inc(s_stack[u][h].handle, 16)

                if active[0]:
                    sp.wait_ge(cF["f_p2"].handle, cF["f_p2"].at(t, 2))
                    sp.wait_ge(cF["f_p3"].handle, cF["f_p3"].at(t, 2))
                    for h in range(2):
                        sp.wait_ge(s_stack[u][h].handle, s_stack[u][h].at(half - 1, 192))
                    for pair in range(PAIRS):
                        sp.dma_start(parts_d[u][:, :, :, pair, :].rearrange("s par d t -> (par d) s t"),
                                     parts[2 * HD * pair:2 * HD * (pair + 1), :, :]).then_inc(s_parts[u].handle, 16)
                    sp.wait_ge(s_parts[u].handle, s_parts[u].at(half, 16 * PAIRS))
                if active[2]:
                    sp.wait_ge(cF["f_ST"].handle, cF["f_ST"].at(t - 2, 32))
                if active[0]:
                    stack(0)
                if active[2]:
                    sp.wait_ge(cF["f_ST"].handle, cF["f_ST"].at(t - 2, 64))
                if active[0]:
                    stack(1)
            steps(sp, BATCHES, 2, attention_io)

            sp.wait_ge(cF["f_fin"].handle, cF["f_fin"].at(BATCHES - 1, 1))
            expert_io(1)
            od = out.rearrange("b (t p) d -> p (b t) d", p=P)

            def store(t, u, half, active):
                sp.wait_ge(cG[1].handle, cG[1].at(t, 1))
                sp.dma_start(od[:, tiles_of(t), :], X[:, tiles_of(t), :]).then_inc(s_out, 16)
            steps(sp, BATCHES, 0, store)
            sp.wait_ge(s_out, 16 * BATCHES)

        @block.gpsimd
        def _(pool):
            for c in counts_by_engine["pool"]:
                c.start(pool)
            g = nc.gpsimd
            pool_e = pool.alloc_register("pool_expert")
            g.memset(zeros512[:, :], 0.0).then_inc(s_cst, 1)
            g.memset(ident[:, :], 0.0)
            g.memset(ones512[:, :], 1.0)
            g.memset(onesb[:, :], 1.0)
            g.memset(blk[:, :], 1.0)
            g.memset(maskS[:, :], 0.0)
            g.memset(rt[:, 0, 0:P], 0.0)
            g.memset(vaug[:, :, :], 0.0)
            g.iota(EID[:, :], pattern=[[1, SLOT_TILES]], base=0, channel_multiplier=0)
            g.iota(rs8i[:, :], pattern=[[-1, E]], base=E, channel_multiplier=0)
            pool.drain()
            g.tensor_copy(iotaJ[:, :], EID[:, :])
            g.tensor_copy(iotaE[:, :], rs8i[:, :])
            g.affine_select(out=ident[:, :], in_=ident[:, :], compare_op=ALU.not_equal, fill=1.0, base=0,
                            pattern=[[-1, P]], channel_multiplier=1)
            g.affine_select(out=tri[:, :], in_=onesb[:, :], compare_op=ALU.is_gt, fill=0.0, base=0,
                            pattern=[[1, P]], channel_multiplier=-1)
            g.affine_select(out=maskT[:, :], in_=rt[:, 0, 0:P], compare_op=ALU.is_ge, fill=LOW, base=0,
                            pattern=[[1, P]], channel_multiplier=-1)
            g.affine_select(out=maskS[:, SEQ - P:], in_=maskS[:, SEQ - P:], compare_op=ALU.is_ge, fill=LOW, base=0,
                            pattern=[[-1, P]], channel_multiplier=1)
            bv3 = blk[:, :].rearrange("p (h d) -> p h d", h=HEADS)
            g.affine_select(out=bv3, in_=bv3, compare_op=ALU.is_ge, fill=0.0, base=0,
                            pattern=[[-HD, HEADS], [0, HD]], channel_multiplier=1)
            pool.drain()
            g.affine_select(out=bv3, in_=bv3, compare_op=ALU.is_ge, fill=0.0, base=HD - 1,
                            pattern=[[HD, HEADS], [0, HD]], channel_multiplier=-1)
            for u in range(2):
                one_col = vaug[:, u, :].rearrange("p (th c) -> p th c", c=32)[:, :, HD:HD + 1]
                g.memset(one_col, 1.0)
            pool.drain()
            g.tensor_copy(identb[:, :], ident[:, :]).then_inc(s_cst, 1)

            def scatter(l, k, u, half):
                pool.nop(nofuse=True)
                for t in range(TPB):
                    g.indirect_dma_start(sorted_x[:, :], bass.IndirectOffsetOnAxis(ap=idx[:, u, t:t + 1], axis=0),
                                         xr[:, u, t * D:(t + 1) * D], None).then_inc(s_scat[l][u].handle, 16)

            def scaled_rows(k, u):
                g.tensor_tensor(v3(xr[:, u, :], TPB), v3(xs[:, u, :], TPB),
                                R2[:, tiles_of(k)].unsqueeze(2).to_broadcast([P, TPB, D]), ALU.mult)
                return g.tensor_copy(idx[:, u, :], POS[:, tiles_of(k)])

            pool.wait_ge(s_route, 1)
            pool.wait_ge(s_zd, 16 * (SLOT_TILES // TPB))

            def layer0(t, u, half, active):
                pool.wait_ge(cC["c_xs"].handle, cC["c_xs"].at(t, 1))
                pool.wait_ge(s_scat[0][u].handle, s_scat[0][u].at(half - 1, 64))
                scaled_rows(t, u).then_inc(cC["c_xr"].handle, 1)
                pool.wait_ge(cC["c_xr"].handle, cC["c_xr"].at(t, 1))
                scatter(0, t, u, half)
            steps(pool, BATCHES, 0, layer0, 2)

            def stage_weights(l):
                c = cD[l]

                def step(t, u, half, active):
                    pool.wait_ge(c["d_h"].handle, c["d_h"].at(t - 2, 2))
                    e = expert_of(pool, pool_e, EID, t * 2)
                    pool.nop(nofuse=True)
                    g.tensor_copy(w1e[u][:, 0:F], W1s[:, bass.ds(e * F, F)]).then_inc(c["d_w"].handle, 1)
                steps(pool, PAIR_STEPS, 0, step)

            pool.wait_ge(cC["c_x"].handle, cC["c_x"].at(BATCHES - 1, 1))
            pool.wait_ge(s_g0, 1)
            pool.wait_ge(s_wf0, 16 * 9)
            stage_weights(0)

            def gather(l):
                for u in range(2):
                    pool.wait_ge(s_yout[l][u].handle, s_yout[l][u].at(PAIR_STEPS // 2 - 1, 16))
                    pool.wait_ge(s_scat[l][u].handle, s_scat[l][u].at(BATCHES // 2 - 1, 64))

                def step(t, u, half, active):
                    pool.wait_ge(cG[l].handle, cG[l].at(t - 2, 1))
                    pool.wait_ge(s_gat[l][u].handle, s_gat[l][u].at(half - 1, 64))
                    pool.nop(nofuse=True)
                    g.tensor_copy(idx[:, u, :], POS[:, tiles_of(t)]).then_inc(c_idx[l].handle, 1)
                    pool.wait_ge(c_idx[l].handle, c_idx[l].at(t, 1))
                    pool.nop(nofuse=True)
                    for j in range(TPB):
                        g.indirect_dma_start(yg[:, u, j * D:(j + 1) * D], None, sorted_y[:, :],
                                             bass.IndirectOffsetOnAxis(ap=idx[:, u, j:j + 1], axis=0)) \
                            .then_inc(s_gat[l][u].handle, 16)
                steps(pool, BATCHES, 0, step, 2)
            gather(0)

            pool.wait_ge(cG[0].handle, cG[0].at(BATCHES - 1, 1))
            for u in range(2):
                g.memset(kst[u], 1.0)
                ins = g.memset(qst[u], 0.0)
            ins.then_inc(s_one, 1)
            pool.wait_ge(s_route, 2)
            for u in range(2):
                pool.wait_ge(s_gat[0][u].handle, s_gat[0][u].at(BATCHES // 2 - 1, 64))

            def layer1(t, u, half, active):
                if active[0]:
                    over = lambda a: a.to_broadcast([P, TPB, D])
                    pool.wait_ge(cF["f_A"].handle, cF["f_A"].at(t - 2, 1))
                    pool.wait_ge(cF["f_xadd"].handle, cF["f_xadd"].at(t - 2, 1))
                    g.tensor_tensor(v3(xs[:, u, :], TPB), X[:, tiles_of(t), :], over(MV[:, tiles_of(t), 0:1]),
                                    ALU.subtract).then_inc(cF["f_xc"].handle, 1)
                    pool.wait_ge(cF["f_xc"].handle, cF["f_xc"].at(t, 1))
                    g.tensor_tensor(v3(xs[:, u, :], TPB), v3(xs[:, u, :], TPB), over(RS[:, tiles_of(t)].unsqueeze(2)),
                                    ALU.mult).then_inc(cF["f_xs"].handle, 1)
                if active[1]:
                    w = (u + 1) % 2
                    pool.wait_ge(cF["f_Ae"].handle, cF["f_Ae"].at(t - 1, 5))
                    pool.wait_ge(cF["f_PV"].handle, cF["f_PV"].at(t - 3, 64))
                    pool.nop(nofuse=True)
                    g.tensor_copy(vaug[:, w, :].rearrange("p (t h r) -> p t h r", t=TPB, r=32)[:, :, :, 0:HD],
                                  vst.rearrange("p t (h d) -> p t h d", d=HD)).then_inc(cF["f_va"].handle, 1)
                if active[0]:
                    pool.wait_ge(cF["f_ms"].handle, cF["f_ms"].at(t - 1, 2))
                    for i in range(2):
                        pool.wait_ge(cF["f_Ae"].handle, cF["f_Ae"].at(t, 3 + 2 * i))
                        qk = raw[:, 2 * i:2 * i + 2, 0:256]
                        g.tensor_tensor(v3(sq[:, 512 * i:512 * i + 512], 2), qk, qk, ALU.mult) \
                            .then_inc(cF["f_sq"].handle, 1)
                if active[3]:
                    pool.wait_ge(cF["f_att"].handle, cF["f_att"].at(t - 3, 4))
                    g.tensor_tensor(X[:, tiles_of(t - 3), :], X[:, tiles_of(t - 3), :], v3(att, TPB), ALU.add) \
                        .then_inc(cF["f_fin"].handle, 1)
                if active[0]:
                    pool.wait_ge(cF["f_ms"].handle, cF["f_ms"].at(t, 3))
                    for i in range(3):
                        if i:
                            pool.wait_ge(cF["f_nw"].handle, cF["f_nw"].at(t, 4 * i))
                        g.tensor_tensor(rt1, rq, rq, ALU.mult).then_inc(cF["f_nw"].handle, 1)
                        pool.wait_ge(cF["f_nw"].handle, cF["f_nw"].at(t, 4 * i + 1))
                        g.tensor_tensor(rt1, rt1, ms, ALU.mult).then_inc(cF["f_nw"].handle, 1)
                        pool.wait_ge(cF["f_nw"].handle, cF["f_nw"].at(t, 4 * i + 2))
                        pool.nop(nofuse=True)
                        g.tensor_scalar(rt1, rt1, -0.5, 1.5, ALU.mult, ALU.add).then_inc(cF["f_nw"].handle, 1)
                        pool.wait_ge(cF["f_nw"].handle, cF["f_nw"].at(t, 4 * i + 3))
                        g.tensor_tensor(rq, rq, rt1, ALU.mult).then_inc(cF["f_nw"].handle, 1)
                    pool.wait_ge(cF["f_kn0"].handle, cF["f_kn0"].at(t, 1))
                    k3 = kn.rearrange("p (n d) -> p n d", d=HD)
                    g.tensor_tensor(k3, k3, kwbc[:, :].unsqueeze(1).to_broadcast([P, SEQ // HD, HD]),
                                    ALU.mult).then_inc(cF["f_kw"].handle, 1)
                    pool.wait_ge(cF["f_kw"].handle, cF["f_kw"].at(t, 1))
                    g.tensor_tensor(v3(kn, TPB), v3(kn, TPB), raw[:, :, 256:384], ALU.add) \
                        .then_inc(cF["f_kn"].handle, 1)
                    for a in range(2):
                        pool.wait_ge(cF["f_p2"].handle, cF["f_p2"].at(t, a + 1))
                        g.tensor_tensor(parts[:, 3 * a + 2, :], r1[:, a, :], parts[:, 3 * a + 1, :],
                                        ALU.subtract).then_inc(cF["f_p3"].handle, 1)
                if active[0]:
                    pool.wait_ge(cF["f_xs"].handle, cF["f_xs"].at(t, 1))
                    pool.wait_ge(s_scat[1][u].handle, s_scat[1][u].at(half - 1, 64))
                    scaled_rows(t, u).then_inc(cF["f_xr"].handle, 1)
                    g.tensor_tensor(X[:, tiles_of(t), :], X[:, tiles_of(t), :], v3(xs[:, u, :], TPB),
                                    ALU.add).then_inc(cF["f_xadd"].handle, 1)
                    pool.wait_ge(cF["f_xr"].handle, cF["f_xr"].at(t, 1))
                    scatter(1, t, u, half)
            steps(pool, BATCHES, 3, layer1)
            pool.wait_ge(cF["f_att"].handle, cF["f_att"].at(BATCHES - 1, 4))
            pool.wait_ge(s_g1, 1)
            stage_weights(1)
            gather(1)

        @block.vector
        def _(dve):
            for c in counts_by_engine["dve"]:
                c.start(dve)
            v = nc.vector
            dve_e = [dve.alloc_register(f"dve_expert{i}") for i in range(2)]

            def tt(out, a, b, op):
                return v.tensor_tensor(out, a, b, op)

            dve.wait_ge(s_cst, 2)
            dve.wait_ge(s_w, N_W)
            v.tensor_scalar(sqblk[:, :], blk[:, :], -0.5 / HD, None, ALU.mult).then_inc(s_set_dv, 1)
            dve.wait_ge(s_set_pe, 1)
            v.tensor_copy(wT[:, :, :].rearrange("p a b -> p (a b)"), bank[0][:, :])
            v.tensor_copy(glT[:, :, :].rearrange("p a b -> p (a b)"), bank[1][:, 0:2 * E])
            v.tensor_copy(gbT[:, :], bank[1][:, 16:16 + 2 * E])
            v.tensor_copy(b1T[:, :], bank[1][:, 32:32 + E * FC])
            rep = lambda src, n: src.unsqueeze(1).to_broadcast([n, HEADS, HD])
            r3 = lambda i, n: wrep[0:n, i, :].rearrange("p (h d) -> p h d", h=HEADS)
            v.tensor_copy(r3(0, 64), rep(wsm[0:64, 0, 0:HD], 64))
            v.tensor_copy(r3(1, 64), rep(bank[1][0:64, 64:64 + HD], 64))
            v.tensor_copy(r3(2, P), rep(wsm[:, 2, 0:HD], P))
            v.tensor_copy(r3(3, P), rep(bank[1][:, 72:72 + HD], P))
            v.tensor_copy(r3(4, 64), rep(wsm[0:64, 0, HD:2 * HD], 64))
            v.tensor_copy(r3(5, 64), rep(wsm[0:64, 0, 2 * HD:3 * HD], 64))
            v.tensor_copy(r3(6, HD), rep(bank[1][0:HD, 88:88 + HD], HD))
            v.tensor_copy(wsm[0:HD, 1, :].rearrange("p (h d) -> p h d", h=HEADS),
                          rep(ident[0:HD, 0:HD], HD)).then_inc(s_set_dv, 1)
            dve.wait_ge(s_set_pe, 2)
            v.tensor_copy(wrep[:, 7, :], bank[2][:, 0:P]).then_inc(s_set_dv, 1)
            rcol = bank[2][:, P:P + HD].unsqueeze(1).to_broadcast([P, HEADS, HD])
            b3 = lambda ap: ap.rearrange("p (h d) -> p h d", h=HEADS)
            tt(b3(Rblk[:, :]), rcol, b3(blk[:, :]), ALU.mult)
            v.tensor_scalar(vecs[:, 3:4], bank[2][:, 136:137], HD ** -0.5, None, ALU.mult)
            v.tensor_scalar(glT[:, 0, :], glT[:, 0, :], vecs[:, 2:3], None, ALU.mult)
            dve.drain()
            v.tensor_scalar(Rblk[:, :], Rblk[:, :], HD ** -0.5, None, ALU.mult)
            dve.wait_ge(s_set_pe, 3)
            for i in range(4):
                ins = tt(PROJ[:, i * P:(i + 1) * P], bank[3][:, i * P:(i + 1) * P], blk[:, :], ALU.mult)
            ins.then_inc(s_set_dv, 1)

            def stats_of_batch(k):
                for t in range(TPB):
                    v.bn_stats(st6[:, t, :], X[:, k * TPB + t, :])
                dve.drain()
                for t in range(TPB):
                    v.bn_aggr(mv4[:, t, :], st6[:, t, :])
                dve.drain()
                return v.tensor_copy(MV[:, tiles_of(k), :], mv4[:, :, :])

            def rsqrt64(dst, src):
                dve.drain()
                v.tensor_scalar(rsi[:, :], src.bitcast(I32), 1, None, ALU.arith_shift_right)
                dve.drain()
                v.tensor_scalar(dst.bitcast(I32), rsi[:, :], -1.0, RSQRT_GUESS, ALU.mult, ALU.add)
                dve.drain()
                for _step in range(3):
                    tt(tmp64[:, 2, :], dst, dst, ALU.mult)
                    dve.drain()
                    v.scalar_tensor_tensor(out=tmp64[:, 2, :], in0=tmp64[:, 2, :], scalar=-0.5, op0=ALU.mult,
                                           in1=src, op1=ALU.mult)
                    dve.drain()
                    v.scalar_tensor_tensor(out=dst, in0=tmp64[:, 2, :], scalar=1.5, op0=ALU.add,
                                           in1=dst, op1=ALU.mult)
                    dve.drain()

            def norms(eps2):
                dve.drain()
                v.tensor_scalar(tmp64[:, 3, :], MV[:, :, 1], LN_EPS, None, ALU.add)
                rsqrt64(RS[:, :], tmp64[:, 3, :])
                tt(tmp64[:, 3, :], RS[:, :], RS[:, :], ALU.mult)
                dve.drain()
                tt(tmp64[:, 3, :], tmp64[:, 3, :], MV[:, :, 1], ALU.mult)
                dve.drain()
                v.tensor_scalar(tmp64[:, 3, :], tmp64[:, 3, :], eps2, None, ALU.add)
                rsqrt64(R2[:, :], tmp64[:, 3, :])

            def normalize(k, u):
                over = lambda a: a.to_broadcast([P, TPB, D])
                tt(v3(xs[:, u, :], TPB), X[:, tiles_of(k), :], over(MV[:, tiles_of(k), 0:1]), ALU.subtract)
                dve.drain()
                return tt(v3(xs[:, u, :], TPB), v3(xs[:, u, :], TPB), over(RS[:, tiles_of(k)].unsqueeze(2)), ALU.mult)

            def route(l):
                dve.drain()
                dve.wait_ge(cB[l]["b_lgc"].handle, cB[l]["b_lgc"].at(BATCHES - 1, 1))
                dve.wait_ge(s_gsum, l + 1)
                wide = lambda a: a.to_broadcast([P, TILES, E])
                means = rt[:, 0, :].rearrange("p (t e) -> p t e", e=E)
                tt(means, wide(MV[:, :, 0:1]), wide(bank[4][:, 0:E].unsqueeze(1)), ALU.mult)
                if l == 0:
                    tt(tmp64[:, 3, :], RS[:, :], R2[:, :], ALU.mult)
                dve.drain()
                tt(LG[:, :, :], LG[:, :, :], means, ALU.subtract)
                dve.drain()
                m = tmp64[:, 0, :]
                v.tensor_reduce(m, LG[:, :, :], AX_X, ALU.max)
                dve.drain()
                bc = lambda a: a.unsqueeze(2).to_broadcast([P, TILES, E])
                t3 = lambda i: rt[:, i, :].rearrange("p (t e) -> p t e", e=E)
                tt(t3(0), LG[:, :, :], bc(m), ALU.is_ge)
                dve.drain()
                tt(t3(0), t3(0), iotaE[:, :].unsqueeze(1).to_broadcast([P, TILES, E]), ALU.mult)
                dve.drain()
                v.tensor_reduce(tmp64[:, 1, :], t3(0), AX_X, ALU.max)
                if l == 0:
                    tt(t3(1), LG[:, :, :], bc(m), ALU.subtract)
                    dve.drain()
                    tt(t3(2), t3(1), bc(tmp64[:, 3, :]), ALU.mult).then_inc(s_rt_dv, 1)
                else:
                    dve.drain()
                    tt(tmp64[:, 2, :], m, RS[:, :], ALU.mult).then_inc(s_rt_dv, 1)
                dve.drain()
                tt(ohE[:, :, :].rearrange("p e t -> p t e"), t3(0), bc(tmp64[:, 1, :]), ALU.is_equal) \
                    .then_inc(s_rt_dv, 1)
                dve.wait_ge(s_rt_ac, l + 1)
                if l == 0:
                    v.tensor_reduce(tmp64[:, 3, :], t3(2), AX_X, ALU.add)
                else:
                    v.tensor_scalar(tmp64[:, 3, :], tmp64[:, 2, :], 1.0, None, ALU.add)
                dve.drain()
                v.reciprocal(SC[:, :], tmp64[:, 3, :])
                dve.wait_ge(s_rt_pe, l + 1)
                cnt, rank = bank[0][:, :], bank[1][:, :]
                cum = rt[:, 1, :]
                v.tensor_tensor_scan(cum, ones512[:, :], cnt, 0.0, ALU.mult, ALU.add)
                dve.drain()
                cum3 = cum.rearrange("p (e t) -> p e t", e=E)
                v.tensor_copy(rs8[:, 0, :], cum3[:, :, TILES - 1])
                tt(rt[:, 2, :], cum, cnt, ALU.subtract)
                v.memset(rs8[:, 1, 0:1], 0.0)
                dve.drain()
                v.tensor_copy(rs8[:, 1, 1:E], rs8[:, 0, 0:E - 1])
                tt(rt[:, 2, :], rt[:, 2, :], rank, ALU.add)
                dve.drain()
                tt(rs8[:, 2, :], rs8[:, 0, :], rs8[:, 1, :], ALU.subtract)
                dve.drain()
                v.tensor_scalar(rs8[:, 2, :], rs8[:, 2, :], float(P - 1), None, ALU.add)
                dve.drain()
                v.tensor_copy(rs8i[:, :], rs8[:, 2, :])
                dve.drain()
                v.tensor_scalar(rs8i[:, :], rs8i[:, :], P.bit_length() - 1, None, ALU.arith_shift_right)
                dve.drain()
                v.tensor_copy(rs8[:, 3, :], rs8i[:, :])
                dve.drain()
                v.tensor_tensor_scan(rs8[:, 4, :], ones512[:, 0:E], rs8[:, 3, :], 0.0, ALU.mult, ALU.add)
                dve.drain()
                tt(rs8[:, 5, :], rs8[:, 4, :], rs8[:, 3, :], ALU.subtract)
                tt(rj[:, :, :], iotaJ[:, :].unsqueeze(2).to_broadcast([P, SLOT_TILES, E]),
                   rs8[:, 4, :].unsqueeze(1).to_broadcast([P, SLOT_TILES, E]), ALU.is_ge)
                dve.drain()
                v.tensor_reduce(rjs[:, :], rj[:, :, :], AX_X, ALU.add)
                v.tensor_scalar(rs8[:, 6, :], rs8[:, 5, :], float(P), None, ALU.mult)
                dve.drain()
                v.tensor_scalar(rjs[:, :], rjs[:, :], float(E - 1), None, ALU.min)
                tt(rs8[:, 7, :], rs8[:, 6, :], rs8[:, 1, :], ALU.subtract)
                dve.drain()
                v.tensor_copy(EID[:, :], rjs[:, :])
                e3 = lambda i: rt[:, i, :].rearrange("p (e t) -> p e t", e=E)
                tt(e3(2), e3(2), rs8[:, 7, :].unsqueeze(2).to_broadcast([P, E, TILES]), ALU.add)
                dve.drain()
                tt(e3(2), e3(2), ohE[:, :, :], ALU.mult)
                dve.drain()
                v.tensor_reduce(tmp64[:, 0, :], rt[:, 2, :].rearrange("p (e t) -> p t e", e=E), AX_X, ALU.add)
                dve.drain()
                v.tensor_copy(POS[:, :], tmp64[:, 0, :]).then_inc(s_route, 1)

            for i in range(X_LOADS):
                dve.wait_ge(s_x[i], 16)
                first = i * (BATCHES // X_LOADS)
                steps(dve, BATCHES // X_LOADS, 0, lambda t, u, half, active, first=first:
                      stats_of_batch(t + first).then_inc(c_stat.handle, 1))
            norms(RMS_EPS0)
            route(0)
            def attention0(t, u, half, active):
                c = cC
                a, b, k, w = t - 1, t - 2, t - 3, (u + 1) % 2

                def at(name, i):
                    dve.wait_ge(c[name].handle, c[name].at(i, 1))

                if active[0]:
                    at("c_T", t - 2)
                    at("c_xr", t - 2)
                    normalize(t, u).then_inc(c["c_xs"].handle, 1)
                if active[3]:
                    at("c_kv", k)
                    tt(kvm, bank[7][:, 0:P], blk[:, :], ALU.mult).then_inc(c["c_kvm"].handle, 1)
                    at("c_qzT", k)
                    v.tensor_copy(qzT, bank[6][:, :]).then_inc(c["c_qzTc"].handle, 1)
                    at("c_kvo", k)
                    v.tensor_copy(kvo, bank[7][:, P:2 * P]).then_inc(c["c_kvoc"].handle, 1)
                if active[2]:
                    at("c_exp", b)
                    q3 = qp.rearrange("p (n d) -> p n d", d=HD)
                    v.tensor_reduce(qs, q3, AX_X, ALU.add)
                    dve.drain()
                    v.tensor_scalar(qs, qs, 1e-8, None, ALU.add)
                    dve.drain()
                    v.reciprocal(qr, qs)
                    dve.drain()
                    at("c_qzT", b - 1)
                    tt(qz.rearrange("p (n d) -> p n d", d=HD), q3,
                       qr.unsqueeze(2).to_broadcast([P, TPB * HEADS, HD]), ALU.mult).then_inc(c["c_qz"].handle, 1)
                if active[1]:
                    at("c_qkv", a)
                    at("c_kv", a - 2)
                    tt(v3(v_s[w], TPB), v3(bank[3][:, :], TPB),
                       bvo[:, 0, :].unsqueeze(1).to_broadcast([P, TPB, D]), ALU.add).then_inc(c["c_v"].handle, 1)
                if active[3]:
                    at("c_o", k)
                    tt(v3(ot, TPB), v3(bank[6][:, :], TPB),
                       bvo[:, 1, :].unsqueeze(1).to_broadcast([P, TPB, D]), ALU.add).then_inc(c["c_or"].handle, 1)
                    dve.drain()
                    tt(X[:, tiles_of(k), :], X[:, tiles_of(k), :], v3(ot, TPB), ALU.add) \
                        .then_inc(c["c_x"].handle, 1)
            steps(dve, BATCHES, 3, attention0)

            def experts(l):
                c = cD[l]

                def step(t, u, half, active):
                    if active[1]:
                        k, w = t - 1, (u + 1) % 2
                        dve.wait_ge(c["d_ha"].handle, c["d_ha"].at(k - 2, 1))
                        for i in range(2):
                            e = expert_of(dve, dve_e[i], EID, k * 2 + i)
                            dve.wait_ge(c["d_h"].handle, c["d_h"].at(k, i + 1))
                            tt(v3(hb[w][:, i * F:(i + 1) * F], FC), v3(bank[1 + 2 * w + i][:, :], FC),
                               b1T[:, bass.ds(e * FC, FC)].unsqueeze(2).to_broadcast([P, FC, P]), ALU.add) \
                                .then_inc(c["d_hb"].handle, 1)
                    if active[2]:
                        k = t - 2
                        dve.wait_ge(s_yout[l][u].handle, s_yout[l][u].at(half - 2, 16))
                        for i in range(2):
                            e = expert_of(dve, dve_e[i], EID, k * 2 + i)
                            if i == 0:
                                dve.wait_ge(c["d_y"].handle, c["d_y"].at(k, 1))
                            ins = tt(ys[u][:, i * D:(i + 1) * D], bank[5 + u][:, i * D:(i + 1) * D],
                                     b2bc[:, bass.ds(e * D, D)], ALU.add)
                        ins.then_inc(c["d_ys"].handle, 1)
                steps(dve, PAIR_STEPS, 2, step)

            def combine(l, with_stats):
                def step(t, u, half, active):
                    dve.wait_ge(s_gat[l][u].handle, s_gat[l][u].at(half, 64))
                    if l == 1:
                        dve.wait_ge(cF["f_fin"].handle, cF["f_fin"].at(t, 1))
                    for j in range(TPB):
                        ins = v.scalar_tensor_tensor(out=X[:, t * TPB + j, :], in0=yg[:, u, j * D:(j + 1) * D],
                                                     scalar=SC[:, bass.ds(t * TPB + j, 1)], op0=ALU.mult,
                                                     in1=X[:, t * TPB + j, :], op1=ALU.add)
                    ins.then_inc(cG[l].handle, 1)
                    if with_stats:
                        dve.drain()
                        stats_of_batch(t)
                steps(dve, BATCHES, 0, step)

            experts(0)
            combine(0, True)

            norms(FFN_EPS1)
            route(1)
            dve.wait_ge(s_set_pe, 4)
            v.tensor_copy(rt[:, 0, 0:E * FC], bank[5][:, 0:E * FC])
            dve.drain()
            tt(b1T[:, :], rt[:, 0, 0:E * FC], bank[6][:, 0:E * FC], ALU.add).then_inc(s_f1, 1)


            def attention1(t, u, half, active):
                c = cF
                a, b, k = t, t - 1, t - 2
                w = (u + 1) % 2

                def at(name, i, n):
                    dve.wait_ge(c[name].handle, c[name].at(i, n))

                def maximum(n):
                    h, qt = n // TPB, n % TPB
                    width = (qt + 1) * P
                    at("f_S", b, n + 1)
                    at("f_mx", b, n - 1)
                    dve.nop(nofuse=True)
                    v.tensor_tensor_reduce(out=junk[:, n % 2, 0:width], in0=bank[n % 2][:, 0:width],
                                           in1=maskS[:, SEQ - width:], scale=1.0, scalar=3 * LOW,
                                           op0=ALU.add, op1=ALU.max, accum_out=MX[:, qt * HEADS + h:qt * HEADS + h + 1]) \
                        .then_inc(c["f_mx"].handle, 1)

                def max_parts(k, h, stage):
                    m3 = MX.rearrange("p (q h) -> p q h", q=TPB)[:, :, 8 * h:8 * h + 8]
                    r = [mr[:, 32 * i:32 * i + 32].rearrange("p (q h) -> p q h", q=TPB) for i in range(2)]
                    mp = mparts[:, 96 * h:96 * h + 96].rearrange("p (q s h) -> p q s h", q=TPB, s=3)
                    if stage == 0:
                        v.tensor_scalar(r[0], m3, -1.0, None, ALU.mult)
                    if stage == 1:
                        at("f_mT", k - 1, h + 1)
                        v.tensor_copy(mp[:, :, 0, :], r[0])
                    if stage == 2:
                        tt(r[1], r[0], mp[:, :, 0, :], ALU.subtract)
                    if stage == 3:
                        v.tensor_copy(mp[:, :, 1, :], r[1])
                    if stage == 4:
                        tt(mp[:, :, 2, :], r[1], mp[:, :, 1, :], ALU.subtract).then_inc(c["f_mp"].handle, 1)

                def prepare(n):
                    if n in (13, 16):
                        i = 0 if n == 13 else 1
                        at("f_sq", a, i + 1)
                        v.tensor_reduce(ms[:, 64 * i:64 * i + 64],
                                        sq[:, 512 * i:512 * i + 512].rearrange("p (n d) -> p n d", d=HD),
                                        AX_X, ALU.add).then_inc(c["f_ms"].handle, 1)
                    if n == 17:
                        at("f_ms", a, 2)
                        v.tensor_scalar(ms, ms, 1.0 / HD, RMS_EPS1, ALU.mult, ALU.add)
                        dve.drain()
                        v.tensor_scalar(rgi, ms.bitcast(I32), 1, None, ALU.arith_shift_right)
                        dve.drain()
                        v.tensor_scalar(rq.bitcast(I32), rgi, -1.0, RSQRT_GUESS, ALU.mult, ALU.add) \
                            .then_inc(c["f_ms"].handle, 1)
                    if n in (24, 25):
                        i = 1 if n == 24 else 0
                        dst = kn if i else qn
                        at("f_nw", a, 12)
                        if i:
                            at("f_A", a - 1, 7)
                        r4 = rq.rearrange("p (t a h) -> p a t h", t=TPB, a=2)
                        src = raw[:, :, 128 * i:128 * i + 128].rearrange("p t (h d) -> p t h d", d=HD)
                        tt(dst.rearrange("p (t h d) -> p t h d", t=TPB, d=HD), src,
                           r4[:, i].unsqueeze(3).to_broadcast([P, TPB, HEADS, HD]), ALU.mult) \
                            .then_inc(c["f_kn0" if i else "f_qn"].handle, 1)
                    if n in (32, 36):
                        i = 0 if n == 32 else 1
                        at("f_p1", a, i + 1)
                        at("f_p3", a - 1, 2)
                        src = bank[6][:, :]
                        if i == 0:
                            v.scalar_tensor_tensor(out=r1[:, 0, :], in0=src, scalar=vecs[:, 3:4], op0=ALU.mult,
                                                   in1=parts[:, 0, :], op1=ALU.subtract).then_inc(c["f_r1"].handle, 1)
                        else:
                            tt(r1[:, 1, :], src, parts[:, 3, :], ALU.subtract).then_inc(c["f_r1"].handle, 1)

                def denominators(k, qd):
                    at("f_OT", k, qd + 1)
                    o4 = bank[7][:, :].rearrange("p (t j r) -> p t j r", t=TPB, r=32)
                    v.reciprocal(rden.rearrange("p (t j) -> p t j", t=TPB), o4[:, :, :, HD])

                def normalized_output(k, qd):
                    o4 = bank[7][:, :].rearrange("p (t j r) -> p t j r", t=TPB, r=32)
                    if qd == 0:
                        at("f_fin", k - 1, 1)
                    tt(att.rearrange("p (t g j d) -> p t g j d", t=TPB, g=QUADS, d=HD)[:, :, qd],
                       o4[:, :, :, 0:HD], rden.rearrange("p (t j) -> p t j", t=TPB).unsqueeze(3)
                       .to_broadcast([P, TPB, 4, HD]), ALU.mult).then_inc(c["f_att"].handle, 1)

                for n in range(64):
                    if active[1]:
                        maximum(n)
                    else:
                        dve.drain()
                    if active[0]:
                        prepare(n)
                    if active[1] and n in (34, 37, 40, 43, 46):
                        max_parts(b, 0, (n - 34) // 3)
                    if active[2] and n in (2, 5, 8, 11, 14):
                        max_parts(k, 1, (n - 2) // 3)
                    for back, ready in ((3, n < 16), (2, n >= 16)):
                        if active[back] and ready and n % 16 == 9:
                            denominators(t - back, (n // 16 - 1) % QUADS)
                        if active[back] and ready and n % 16 == 12:
                            normalized_output(t - back, (n // 16 - 1) % QUADS)
            steps(dve, BATCHES, 3, attention1)
            experts(1)
            combine(1, False)

        @block.scalar
        def _(act):
            for c in counts_by_engine["act"]:
                c.start(act)
            s = nc.scalar
            act_e = act.alloc_register("act_expert")

            def logits(l, ready):
                c = cB[l]

                def step(t, u, half, active):
                    w = (u + 1) % 2
                    if active[0]:
                        act.wait_ge(ready.handle, ready.at(t, 1))
                        act.wait_ge(c["b_T"].handle, c["b_T"].at(t - 2, 1))
                        s.copy(v3(xs[:, u, :], TPB), X[:, tiles_of(t), :]).then_inc(c["b_xs"].handle, 1)
                    if active[1]:
                        act.wait_ge(c["b_T"].handle, c["b_T"].at(t - 1, 1))
                        act.wait_ge(c["b_lg"].handle, c["b_lg"].at(t - 3, 1))
                        s.copy(xT[:, w, :], bank[w][:, :]).then_inc(c["b_xT"].handle, 1)
                    if active[2]:
                        act.wait_ge(c["b_lg"].handle, c["b_lg"].at(t - 2, 1))
                        s.copy(LG[:, tiles_of(t - 2), :],
                               v3(bank[2 + u][:, 0:TPB * E], TPB)).then_inc(c["b_lgc"].handle, 1)
                steps(act, BATCHES, 2, step)

            logits(0, c_stat)
            act.wait_ge(s_rt_dv, 1)
            s.activation(rt[:, 2, :], rt[:, 2, :], ACT.Exp).then_inc(s_rt_ac, 1)
            act.wait_ge(s_wf0, 16 * 9)
            for e in range(E):
                ins = s.activation(W1s[:, e * F:(e + 1) * F], W1s[:, e * F:(e + 1) * F], ACT.Copy, scale=vecs[:, 2:3])
            ins.then_inc(s_g0, 1)

            def attention0(t, u, half, active):
                c = cC
                a, b = t - 1, t - 2
                if active[1]:
                    act.wait_ge(c["c_T"].handle, c["c_T"].at(a, 1))
                    act.wait_ge(c["c_qkv"].handle, c["c_qkv"].at(a - 1, 1))
                    s.copy(xT[:, 0, :], bank[0][:, :]).then_inc(c["c_xT"].handle, 1)
                if active[2]:
                    act.wait_ge(c["c_proj"].handle, c["c_proj"].at(b, 1))
                    act.wait_ge(c["c_kv"].handle, c["c_kv"].at(b - 1, 1))
                    act.wait_ge(c["c_qz"].handle, c["c_qz"].at(b - 1, 1))
                    s.activation(qp, bank[4][:, :], ACT.Exp)
                    s.activation(kp, bank[5][:, :], ACT.Exp).then_inc(c["c_exp"].handle, 1)
                if active[1]:
                    act.wait_ge(c["c_qkv"].handle, c["c_qkv"].at(a, 1))
                    act.wait_ge(c["c_proj"].handle, c["c_proj"].at(a - 1, 1))
                    s.activation(qT, bank[1][:, :], ACT.Identity, bias=vecs[:, 0:1])
                    s.activation(qsq, bank[1][:, :], ACT.Square, bias=vecs[:, 0:1])
                    s.activation(kT, bank[2][:, :], ACT.Identity, bias=vecs[:, 1:2])
                    s.activation(ksq, bank[2][:, :], ACT.Square, bias=vecs[:, 1:2]).then_inc(c["c_qk"].handle, 1)
            steps(act, BATCHES, 2, attention0)

            def experts(l, func):
                c = cD[l]

                def step(t, u, half, active):
                    w = (u + 1) % 2
                    if active[0]:
                        act.wait_ge(c["d_T"].handle, c["d_T"].at(t, 1))
                        act.wait_ge(c["d_h"].handle, c["d_h"].at(t - 2, 2))
                        s.copy(xinT[u], bank[7 * u][:, 0:2 * P]).then_inc(c["d_xT"].handle, 1)
                        e = expert_of(act, act_e, EID, t * 2 + 1)
                        s.copy(w1e[u][:, F:2 * F], W1s[:, bass.ds(e * F, F)]).then_inc(c["d_wo"].handle, 1)
                    if active[1]:
                        k = t - 1
                        act.wait_ge(c["d_hb"].handle, c["d_hb"].at(k, 2))
                        act.wait_ge(c["d_y"].handle, c["d_y"].at(k - 2, 1))
                        s.activation(ha[w], hb[w], func).then_inc(c["d_ha"].handle, 1)
                steps(act, PAIR_STEPS, 1, step)
            experts(0, ACT.Silu)

            logits(1, cG[0])
            act.wait_ge(s_rt_dv, 3)
            s.activation(tmp64[:, 2, :], tmp64[:, 2, :], ACT.Exp, scale=-1.0).then_inc(s_rt_ac, 1)
            act.wait_ge(s_wf1, 16 * 10)
            act.wait_ge(s_set_pe, 4)
            for e in range(E):
                ins = s.activation(W1s[:, e * F:(e + 1) * F], W1s[:, e * F:(e + 1) * F], ACT.Copy,
                                   scale=gbT[:, e:e + 1])
            ins.then_inc(s_g1, 1)
            act.wait_ge(s_route, 2)

            def attention1(t, u, half, active):
                c = cF
                a, b, k = t, t - 1, t - 2
                w = (u + 1) % 2

                def at(name, i, n):
                    act.wait_ge(c[name].handle, c[name].at(i, n))

                def prepare(n):
                    if n == 1:
                        at("f_A", a, 1)
                        at("f_A", a - 1, 5)
                        s.copy(xT[:, 0, :], bank[6][:, :]).then_inc(c["f_Ae"].handle, 1)
                    if n in (4, 7, 10, 13):
                        j = (n - 4) // 3
                        at("f_A", a, j + 2)
                        if j == 0:
                            at("f_kn", a - 1, 1)
                            at("f_qn", a - 1, 1)
                            at("f_va", a - 1, 1)
                        s.copy(raw[:, j, :], bank[6][:, :]).then_inc(c["f_Ae"].handle, 1)
                    if n in (29, 34):
                        i = 0 if n == 29 else 1
                        at("f_A", a, 6 + i)
                        if i == 0:
                            act.wait_ge(s_parts[w].handle, s_parts[w].at(half + u - 1, 16 * PAIRS))
                            s.activation(parts[:, 0, :], bank[6][:, :], ACT.Identity, scale=vecs[:, 3:4]) \
                                .then_inc(cF["f_p1"].handle, 1)
                        else:
                            s.copy(parts[:, 3, :], bank[6][:, :]).then_inc(cF["f_p1"].handle, 1)
                    if n in (33, 37):
                        i = 0 if n == 33 else 1
                        at("f_r1", a, i + 1)
                        s.copy(parts[:, 3 * i + 1, :], r1[:, i, :]).then_inc(c["f_p2"].handle, 1)

                def max_rows(k, h):
                    at("f_mT", k, h + 1)
                    act.wait_ge(s_mrw[h].handle, s_mrw[h].at(k - 1, 16))
                    s.copy(mrowT[h][0:24, :], bank[7][:, 0:256].bitcast(BF16)[0:24, :]) \
                        .then_inc(c["f_mTc"].handle, 1)

                def max_rows_out(k, h):
                    at("f_mTc", k, h + 1)
                    act.wait_ge(s_mrl[h].handle, s_mrl[h].at(k - 1, 32))
                    act.dma_start(mrow_d[h], mrowT[h][0:24, :]).then_inc(s_mrw[h].handle, 16)

                def max_rows_in(k, w, h):
                    act.wait_ge(s_mrw[h].handle, s_mrw[h].at(k, 16))
                    src = mrow_d[h].rearrange("(s pair par) t -> par s pair t", pair=4, par=2)
                    for par in range(2):
                        rows = slice(64 * par + K_STACK, 64 * par + K_FULL)
                        act.dma_start(qst[w][rows, 4 * h:4 * h + 4, :], src[par]).then_inc(s_mrl[h].handle, 16)

                def evacuate_output(k, qd):
                    at("f_PV", k, 16 * qd + 16)
                    at("f_OT", k, qd)
                    s.copy(OTs, bank[4 + qd % 2][:, :]).then_inc(cF["f_O"].handle, 1)

                for n in range(64):
                    if active[0]:
                        prepare(n)
                    if active[2]:
                        at("f_ST", k, n + 1)
                        at("f_PV", k, n - 3)
                        kt = (n % 8) // 2
                        s.activation(Pb[:, n % 4, 0:SEQ - kt * P], bank[2 + n % 2][:, 0:SEQ - kt * P], ACT.Exp) \
                            .then_inc(c["f_P"].handle, 1)
                        if n % 16 == 3 and n > 3:
                            evacuate_output(k, n // 16 - 1)
                        if n == 18:
                            max_rows(k, 1)
                        if n == 19:
                            max_rows_out(k, 1)
                        if n == 23:
                            max_rows_in(k, u, 1)
                    if active[3] and n == 2:
                        evacuate_output(k - 1, 3)
                    if active[1] and n == 51:
                        max_rows(b, 0)
                    if active[1] and n == 52:
                        max_rows_out(b, 0)
                    if active[1] and n == 56:
                        max_rows_in(b, w, 0)
            steps(act, BATCHES, 3, attention1)
            experts(1, ACT.Relu)

        @block.tensor
        def _(pe):
            for c in counts_by_engine["pe"]:
                c.start(pe)
            mm = nc.tensor.matmul
            pe_e = [pe.alloc_register(f"pe_expert{i}") for i in range(2)]

            def product(out, lhsT, rhs, start=True, stop=True, skip=False):
                return mm(out, lhsT, rhs, start=start, stop=stop, skip_group_check=skip)

            def transpose(out, in_, n=P):
                return nc.tensor.transpose(out, in_, ident[0:n, 0:n])

            pe.wait_ge(s_cst, 2)
            pe.wait_ge(s_w, N_W)
            for i in range(4):
                transpose(bank[0][:, i * P:(i + 1) * P], wn[:, i, :])
            for i in range(2):
                transpose(bank[1][:, i * E:(i + 1) * E], gln[:, i, :], E)
            transpose(bank[1][:, 16:16 + 2 * E], gb[:, :], 2 * E)
            transpose(bank[1][:, 32:32 + E * FC], b1L[0][:, :], E * FC)
            transpose(bank[1][0:64, 64:64 + HD], wsm[0:HD, 1, 0:64], HD)
            transpose(bank[1][:, 72:72 + 2 * HD], wsm[0:2 * HD, 3, :], 2 * HD)
            transpose(bank[1][0:HD, 88:88 + HD], wsm[0:HD, 4, 0:HD], HD).then_inc(s_set_pe, 1)
            pe.wait_ge(s_set_dv, 2)
            product(bank[2][:, 0:P], wsm[0:HD, 5, :], wrep[0:HD, 6, :])
            product(bank[2][:, P:P + HD], wsm[0:HD, 1, :], Rn[:, :])
            product(bank[2][:, 136:137], wsm[0:HD, 1, :], nrm8[:, 0:1]).then_inc(s_set_pe, 1)
            pe.wait_ge(s_set_dv, 3)
            product(bank[3][:, P:2 * P], wrep[:, 2, :], wrep[:, 3, :])
            product(bank[3][:, 2 * P:3 * P], wrep[0:64, 5, :], wrep[0:64, 4, :])
            product(bank[3][:, 3 * P:4 * P], wrep[:, 2, :], wrep[:, 7, :])
            product(bank[3][:, 0:P], wrep[0:64, 0, :], wrep[0:64, 1, :]).then_inc(s_set_pe, 1)

            def logits(l):
                c = cB[l]

                def step(t, u, half, active):
                    if active[0]:
                        pe.wait_ge(c["b_xs"].handle, c["b_xs"].at(t, 1))
                        pe.wait_ge(c["b_xT"].handle, c["b_xT"].at(t - 2, 1))
                        for j in range(TPB):
                            ins = transpose(bank[u][:, j * P:(j + 1) * P], xs[:, u, j * D:(j + 1) * D])
                        ins.then_inc(c["b_T"].handle, 1)
                    if active[2]:
                        k, w = t - 2, u
                        pe.wait_ge(c["b_xT"].handle, c["b_xT"].at(k, 1))
                        pe.wait_ge(c["b_lgc"].handle, c["b_lgc"].at(k - 2, 1))
                        for j in range(TPB):
                            ins = product(bank[2 + w][:, j * E:(j + 1) * E], xT[:, w, j * P:(j + 1) * P], glT[:, l, :])
                        ins.then_inc(c["b_lg"].handle, 1)
                product(bank[4][:, 0:E], ones512[:, 0:P], glT[:, l, :]).then_inc(s_gsum, 1)
                steps(pe, BATCHES, 2, step)

            def route(l):
                pe.wait_ge(s_rt_dv, 2 * l + 2)
                oh = ohE[:, :, :].rearrange("p e t -> p (e t)")
                product(bank[0][:, :], onesb[:, :], oh)
                product(bank[1][:, :], tri[:, :], oh).then_inc(s_rt_pe, 1)

            pe.wait_ge(s_set_dv, 4)
            logits(0)
            route(0)
            pe.wait_ge(s_route, 1)

            def attention0(t, u, half, active):
                c = cC
                a, b, k, w = t - 1, t - 2, t - 3, (u + 1) % 2

                def at(name, i):
                    pe.wait_ge(c[name].handle, c[name].at(i, 1))

                if active[1]:
                    at("c_xs", a)
                    at("c_xT", a - 1)
                    for j in range(TPB):
                        ins = transpose(bank[0][:, j * P:(j + 1) * P], xs[:, w, j * D:(j + 1) * D])
                    ins.then_inc(c["c_T"].handle, 1)
                if active[3]:
                    at("c_exp", k)
                    at("c_v", k)
                    at("c_kvoc", k - 1)
                    for j in range(TPB):
                        cols = slice(j * P, (j + 1) * P)
                        ins = product(bank[7][:, 0:P], v_s[w][:, cols], kp[:, cols], start=(j == 0), stop=(j == TPB - 1))
                    ins.then_inc(c["c_kv"].handle, 1)
                    at("c_qz", k)
                    at("c_or", k - 1)
                    for j in range(TPB):
                        ins = transpose(bank[6][:, j * P:(j + 1) * P], qz[:, j * P:(j + 1) * P])
                    ins.then_inc(c["c_qzT"].handle, 1)
                if active[2]:
                    at("c_qk", b)
                    at("c_exp", b - 1)
                    for bk_, lin, squ in ((4, qT, qsq), (5, kT, ksq)):
                        for j in range(TPB):
                            cols = slice(j * P, (j + 1) * P)
                            product(bank[bk_][:, cols], lin[:, cols], Rblk[:, :], stop=False)
                            ins = product(bank[bk_][:, cols], squ[:, cols], sqblk[:, :], start=False)
                    ins.then_inc(c["c_proj"].handle, 1)
                if active[3]:
                    at("c_kvm", k)
                    product(bank[7][:, P:2 * P], kvm, wT[:, 3, :]).then_inc(c["c_kvo"].handle, 1)
                if active[1]:
                    at("c_xT", a)
                    at("c_qk", a - 1)
                    at("c_v", a - 1)
                    product(bank[1][:, :], wT[:, 0, :], xT[:, 0, :])
                    product(bank[2][:, :], wT[:, 1, :], xT[:, 0, :])
                    for j in range(TPB):
                        ins = product(bank[3][:, j * P:(j + 1) * P], xT[:, 0, j * P:(j + 1) * P], wT[:, 2, :])
                    ins.then_inc(c["c_qkv"].handle, 1)
                if active[3]:
                    at("c_kvoc", k)
                    at("c_qzTc", k)
                    for j in range(TPB):
                        ins = product(bank[6][:, j * P:(j + 1) * P], qzT[:, j * P:(j + 1) * P], kvo)
                    ins.then_inc(c["c_o"].handle, 1)
            steps(pe, BATCHES, 3, attention0)

            def experts(l):
                c = cD[l]

                def step(t, u, half, active):
                    w = (u + 1) % 2
                    if active[0]:
                        pe.wait_ge(s_xin[l][u].handle, s_xin[l][u].at(half, 16))
                        pe.wait_ge(c["d_xT"].handle, c["d_xT"].at(t - 2, 1))
                        for i in range(2):
                            ins = transpose(bank[7 * u][:, i * P:(i + 1) * P], xin[u][:, i * D:(i + 1) * D])
                        ins.then_inc(c["d_T"].handle, 1)
                    if active[1]:
                        k = t - 1
                        pe.wait_ge(c["d_xT"].handle, c["d_xT"].at(k, 1))
                        pe.wait_ge(c["d_w"].handle, c["d_w"].at(k, 1))
                        pe.wait_ge(c["d_wo"].handle, c["d_wo"].at(k, 1))
                        pe.wait_ge(c["d_hb"].handle, c["d_hb"].at(k - 2, 2))
                        for i in range(2):
                            for j in range(FC):
                                ins = product(bank[1 + 2 * w + i][:, j * P:(j + 1) * P],
                                              w1e[w][:, i * F + j * P:i * F + (j + 1) * P],
                                              xinT[w][:, i * P:(i + 1) * P])
                            ins.then_inc(c["d_h"].handle, 1)
                    if active[2]:
                        k = t - 2
                        pe.wait_ge(c["d_ys"].handle, c["d_ys"].at(k - 2, 1))
                        for i in range(2):
                            e = expert_of(pe, pe_e[i], EID, k * 2 + i)
                            if i == 0:
                                pe.wait_ge(c["d_ha"].handle, c["d_ha"].at(k, 1))
                            for j in range(FC):
                                ins = product(bank[5 + u][:, i * D:(i + 1) * D],
                                              ha[u][:, i * F + j * P:i * F + (j + 1) * P],
                                              W2s[:, bass.ds(e * (FC * D) + j * D, D)],
                                              start=(j == 0), stop=(j == FC - 1))
                        ins.then_inc(c["d_y"].handle, 1)
                steps(pe, PAIR_STEPS, 2, step)

            pe.wait_ge(cC["c_x"].handle, cC["c_x"].at(BATCHES - 1, 1))
            experts(0)

            logits(1)
            pe.wait_ge(s_wf1, 16 * 10)
            transpose(bank[5][:, 0:E * FC], b1L[1][:, :], E * FC)
            for e in range(E):
                for j in range(FC):
                    ins = product(bank[6][:, e * FC + j:e * FC + j + 1], W1s[:, e * F + j * P:e * F + (j + 1) * P],
                                  gbT[:, E + e:E + e + 1])
            ins.then_inc(s_set_pe, 1)
            route(1)
            pe.wait_ge(s_route, 2)
            pe.wait_ge(s_f1, 1)

            def attention1(t, u, half, active):
                c = cF
                a, b, k = t, t - 1, t - 2
                w = (u + 1) % 2

                def at(name, i, n):
                    pe.wait_ge(c[name].handle, c[name].at(i, n))

                def prepare(n):
                    if n == 0:
                        at("f_xs", a, 1)
                        at("f_r1", a - 1, 2)
                        for j in range(TPB):
                            ins = transpose(bank[6][:, j * P:(j + 1) * P], xs[:, u, j * D:(j + 1) * D])
                        ins.then_inc(c["f_A"].handle, 1)
                    if n in (3, 6, 9, 12):
                        j = (n - 3) // 3
                        at("f_Ae", a, j + 1)
                        product(bank[6][:, :], xT[:, 0, j * P:(j + 1) * P], PROJ[:, :]).then_inc(c["f_A"].handle, 1)
                    if n in (28, 33):
                        if n == 28:
                            at("f_Ae", a, 5)
                            at("f_qn", a, 1)
                            src = qn
                        else:
                            at("f_kn", a, 1)
                            at("f_r1", a, 1)
                            src = kn
                        for j in range(TPB):
                            ins = transpose(bank[6][:, j * P:(j + 1) * P], src[:, j * P:(j + 1) * P])
                        ins.then_inc(c["f_A"].handle, 1)

                def score(n):
                    h, qt = n // TPB, n % TPB
                    r = slice(64 * (h % 2), 64 * (h % 2) + K_STACK)
                    if n in (0, 32):
                        pe.wait_ge(s_stack[w][n // 32].handle, s_stack[w][n // 32].at(half + u - 1, 192))
                    at("f_mx", b, n - 1)
                    product(bank[n % 2][:, 0:(qt + 1) * P], qst[w][r, h // 2, qt * P:(qt + 1) * P],
                            kst[w][r, h // 2, 0:(qt + 1) * P]).then_inc(c["f_S"].handle, 1)

                def score_T(n):
                    pair, kt, par = n // 8, (n % 8) // 2, n % 2
                    r = slice(64 * par, 64 * par + K_FULL)
                    if n in (0, 32):
                        pe.wait_ge(s_mrl[n // 32].handle, s_mrl[n // 32].at(k, 32))
                    at("f_P", k, n - 1)
                    wide = SEQ - kt * P
                    product(bank[2 + par][:, 0:wide], kst[u][r, pair, kt * P:(kt + 1) * P],
                            qst[u][r, pair, kt * P:SEQ], stop=False)
                    product(bank[2 + par][:, 0:P], identb[:, :], maskT[:, :], start=False).then_inc(c["f_ST"].handle, 1)

                def values(n):
                    pair, kt, par = n // 8, (n % 8) // 2, n % 2
                    qd, j = pair // 2, 2 * (pair % 2) + par
                    h = 2 * pair + par
                    at("f_P", k, n + 1)
                    if n == 0:
                        at("f_va", k, 1)
                    if n % 16 == 0:
                        if qd >= 2:
                            at("f_O", k, qd - 1)
                        else:
                            at("f_O", k - 1, qd + 3)
                    va = vaug[:, u, (kt * HEADS + h) * 32:(kt * HEADS + h) * 32 + 32]
                    product(bank[4 + qd % 2][32 * j:32 * j + 32, kt * P:SEQ], va, Pb[:, n % 4, 0:SEQ - kt * P],
                            start=(kt == 0), stop=(kt == TPB - 1), skip=True).then_inc(c["f_PV"].handle, 1)

                def output_T(k, qd):
                    at("f_O", k, qd + 1)
                    at("f_att", k, qd)
                    if qd == 0:
                        at("f_mTc", k, 2)
                    elif qd == 2 and active[1]:
                        at("f_mTc", b, 1)
                    for j in range(TPB):
                        ins = transpose(bank[7][:, j * P:(j + 1) * P], OTs[:, j * P:(j + 1) * P])
                    ins.then_inc(c["f_OT"].handle, 1)

                def max_rows(m, h):
                    at("f_mp", m, h + 1)
                    if h == 0 and active[2]:
                        at("f_att", k, 2)
                    elif h == 0:
                        at("f_mTc", m - 1, 2)
                    elif active[3]:
                        at("f_att", k - 1, 4)
                    else:
                        at("f_mTc", m, 1)
                    mp = mparts[:, 96 * h:96 * h + 96].rearrange("p (q s) -> p q s", q=TPB)
                    pb = bank[7][:, 0:256].bitcast(BF16)
                    for q in range(TPB):
                        ins = nc.tensor.transpose(pb[0:24, q * P:(q + 1) * P], mp[:, q, :], identb[:, :])
                    ins.then_inc(c["f_mT"].handle, 1)

                for n in range(64):
                    if active[2]:
                        if n >= 3:
                            values(n - 3)
                    if active[0]:
                        prepare(n)
                    if active[1]:
                        score(n)
                    if active[2]:
                        score_T(n)
                        if n == 17:
                            max_rows(k, 1)
                        if n % 16 == 5 and n > 5:
                            output_T(k, n // 16 - 1)
                    if active[3] and n == 5:
                        output_T(k - 1, 3)
                    if active[1] and n == 50:
                        max_rows(b, 0)
                if active[2]:
                    for n in range(61, 64):
                        values(n)

            steps(pe, BATCHES, 3, attention1)
            pe.wait_ge(cF["f_att"].handle, cF["f_att"].at(BATCHES - 1, 4))
            experts(1)


_INS = ['L0_attn_x', 'L0_attn_Wq', 'L0_attn_bq', 'L0_attn_Wk', 'L0_attn_bk', 'L0_attn_Wv', 'L0_attn_bv', 'L0_attn_Wo',
        'L0_attn_bo', 'L0_attn_R', 'L0_ffn_rms_w', 'L0_ffn_gate_w', 'L0_ffn_W1', 'L0_ffn_b1', 'L0_ffn_W2', 'L0_ffn_b2',
        'L1_attn_W_DQ', 'L1_attn_W_UQ', 'L1_attn_W_DKV', 'L1_attn_W_UKV', 'L1_attn_W_QR', 'L1_attn_W_KR', 'L1_attn_W_O',
        'L1_attn_q_norm_w', 'L1_attn_k_norm_w', 'L1_ffn_centroids', 'L1_ffn_w1', 'L1_ffn_b1', 'L1_ffn_w2', 'L1_ffn_b2',
        'L1_ffn_gamma', 'L1_ffn_beta']


def kernel(**inputs):
    from concourse import bacc
    from concourse.bass_utils import run_bass_kernel_spmd

    nc = bacc.Bacc("TRN2", target_bir_lowering=False, num_devices=1)
    nc.disable_value_cache = True
    arrays, args = {}, []
    for name in _INS:
        a = np.ascontiguousarray(inputs[name])
        arrays[f"in_{name}"] = a
        args.append(nc.dram_tensor(f"in_{name}", a.shape, mybir.dt.from_np(a.dtype), kind="ExternalInput").ap())
    args.append(nc.dram_tensor("out_x", (BATCHES, SEQ, D), F32, kind="ExternalOutput").ap())
    build(nc, *args)
    r = run_bass_kernel_spmd(nc, [arrays], core_ids=[0])
    return r.results[0]["out_x"]
```
